# Optimizing a Trainium2 kernel written in Bass

```python
import numpy as np
import jax
import jax.numpy as jnp

def _softmax(x, axis=-1):
    return jax.nn.softmax(x, axis=axis)

def _gelu(x):
    return jax.nn.gelu(x, approximate=True)

def _silu(x):
    return jax.nn.silu(x)

def _sigmoid(x):
    return jax.nn.sigmoid(x)

def _layernorm(x, axis=-1, eps=1e-05):
    m = jnp.mean(x, axis=axis, keepdims=True)
    v = jnp.var(x, axis=axis, keepdims=True)
    return (x - m) / jnp.sqrt(v + eps)

def _scatter_add(tgt, idx, src, axis=0):
    return tgt.at[idx].add(src)

def _segment_sum(src, seg, n):
    return jax.ops.segment_sum(src, seg, n)
kernel_name = 'mk_adaln_ffn_d2_seqx_r8_bdd723'

def setup_inputs(seed: int=0):
    np.random.seed(seed)
    _w = jnp.asarray

    def _rec_inputs():
        import jax
        import jax.numpy as jnp
        _rk = jax.random.key(seed)
        x = -0.0003929 + 0.9999 * jax.random.normal(jax.random.fold_in(_rk, 1), (32, 128, 128), jnp.float32)
        _lenS = 128 - jax.random.randint(jax.random.fold_in(_rk, 7), (32,), 0, max(1, 128 // 4) + 1, jnp.int32)
        _lenS2 = 128 - jax.random.randint(jax.random.fold_in(_rk, 8), (32,), 0, max(1, 128 // 4) + 1, jnp.int32)
        itok_B_0_2 = jax.random.randint(jax.random.fold_in(_rk, 11), (32,), 0, 3, jnp.int32)
        itok_B_0_30 = jax.random.randint(jax.random.fold_in(_rk, 12), (32,), 0, 31, jnp.int32)
        return (x, itok_B_0_2, itok_B_0_30)
    x, itok_B_0_2, itok_B_0_30 = _rec_inputs()

    def _L0_cond_setup():
        import jax, jax.numpy as jnp
        import numpy as np
        NEG_INF = -1e+30
        key = jax.random.key(seed)
        k1, k2, k3, k4, k5 = jax.random.split(key, 5)
        B, S, D, A = (16, 128, 128, 32)
        hidden = jax.random.normal(k1, (B, S, D), dtype=jnp.float32)
        W1 = jax.random.normal(k2, (D, A), dtype=jnp.float32) / np.sqrt(D)
        b1 = jax.random.normal(k3, (A,), dtype=jnp.float32) * 0.01
        v = jax.random.normal(k4, (A,), dtype=jnp.float32) / np.sqrt(A)
        prompt_type_ids = jax.random.randint(k5, (B,), 0, 3, dtype=jnp.int32)
        return {'hidden': hidden, 'W1': W1, 'b1': b1, 'v': v, 'prompt_type_ids': prompt_type_ids}
    _L0_cond_all = _L0_cond_setup()
    _L0_cond_in = {k: v for k, v in _L0_cond_all.items() if k in ('W1', 'b1', 'v')}
    del _L0_cond_all

    def _L0_ffn_setup():
        import jax, jax.numpy as jnp
        import numpy as np
        D_MODEL = 128
        HIDDEN = 256
        E_ROUTED = 14
        E_SHARED = 2
        TOP_K = 2
        EPS = 1e-09
        RMS_EPS = 1.1920929e-07

        def _ffn(xn, rw, W1, W2):
            ms = jnp.mean(xn * xn, axis=-1, keepdims=True)
            h = xn * jax.lax.rsqrt(ms + RMS_EPS) * rw
            return jax.nn.silu(h @ W1) @ W2
        key = jax.random.key(seed)
        ks = jax.random.split(key, 9)
        B, T = (2, 128)
        x = jax.random.normal(ks[0], (B, T, D_MODEL), dtype=jnp.float32)
        router_w = jax.random.normal(ks[1], (D_MODEL, E_ROUTED), dtype=jnp.float32) * 0.006
        rms_w = jnp.ones((E_ROUTED, D_MODEL), dtype=jnp.float32)
        w1 = jax.random.normal(ks[2], (E_ROUTED, D_MODEL, HIDDEN), dtype=jnp.float32) * 0.02
        w2 = jax.random.normal(ks[3], (E_ROUTED, HIDDEN, D_MODEL), dtype=jnp.float32) * 0.02
        rms_w_s = jnp.ones((E_SHARED, D_MODEL), dtype=jnp.float32)
        w1_s = jax.random.normal(ks[4], (E_SHARED, D_MODEL, HIDDEN), dtype=jnp.float32) * 0.02
        w2_s = jax.random.normal(ks[5], (E_SHARED, HIDDEN, D_MODEL), dtype=jnp.float32) * 0.02
        return {'x': x, 'router_w': router_w, 'rms_w': rms_w, 'w1': w1, 'w2': w2, 'rms_w_s': rms_w_s, 'w1_s': w1_s, 'w2_s': w2_s}
    _L0_ffn_all = _L0_ffn_setup()
    _L0_ffn_in = {k: v for k, v in _L0_ffn_all.items() if k in ('router_w', 'rms_w', 'w1', 'w2', 'rms_w_s', 'w1_s', 'w2_s')}
    del _L0_ffn_all

    def _L1_cond_setup():
        import jax, jax.numpy as jnp
        import numpy as np
        C, I, O = (32, 128, 128)
        B, T = (64, 64)
        key = jax.random.key(seed)
        kx, kc, kw, kb = jax.random.split(key, 4)
        x = jax.random.normal(kx, (B, T, I), dtype=jnp.float32)
        cat_ids = jax.random.randint(kc, (B,), 0, C)
        W = 0.02 * jax.random.normal(kw, (C, I, O), dtype=jnp.float32)
        b = jnp.zeros((C, O), dtype=jnp.float32)
        return {'x': x, 'cat_ids': cat_ids, 'W': W, 'b': b}
    _L1_cond_all = _L1_cond_setup()
    _L1_cond_in = {k: v for k, v in _L1_cond_all.items() if k in ('W', 'b')}
    del _L1_cond_all

    def _L1_ffn_setup():
        import jax, jax.numpy as jnp
        import numpy as np
        D_MODEL, D_FF, N_EXPERTS, TOP_K = (128, 256, 8, 2)
        B, S = (2, 256)
        key = jax.random.key(seed)
        ks = jax.random.split(key, 6)
        sd = 1.0 / np.sqrt(D_MODEL)
        sf = 1.0 / np.sqrt(D_FF)
        return {'x': jax.random.normal(ks[0], (B, S, D_MODEL), jnp.float32), 'router_w': jax.random.normal(ks[1], (N_EXPERTS, D_MODEL), jnp.float32) * sd, 'gate_w': jax.random.normal(ks[2], (N_EXPERTS, D_MODEL, D_FF), jnp.float32) * sd, 'gate_b': jnp.zeros((N_EXPERTS, D_FF), jnp.float32), 'up_w': jax.random.normal(ks[3], (N_EXPERTS, D_MODEL, D_FF), jnp.float32) * sd, 'up_b': jnp.zeros((N_EXPERTS, D_FF), jnp.float32), 'down_w': jax.random.normal(ks[4], (N_EXPERTS, D_FF, D_MODEL), jnp.float32) * sf, 'down_b': jnp.zeros((N_EXPERTS, D_MODEL), jnp.float32)}
    _L1_ffn_all = _L1_ffn_setup()
    _L1_ffn_in = {k: v for k, v in _L1_ffn_all.items() if k in ('router_w', 'gate_w', 'gate_b', 'up_w', 'up_b', 'down_w', 'down_b')}
    del _L1_ffn_all
    return {'x': x, 'itok_B_0_2': itok_B_0_2, 'itok_B_0_30': itok_B_0_30, 'L0_cond_W1': _L0_cond_in['W1'], 'L0_cond_b1': _L0_cond_in['b1'], 'L0_cond_v': _L0_cond_in['v'], 'L0_ffn_router_w': _L0_ffn_in['router_w'], 'L0_ffn_rms_w': _L0_ffn_in['rms_w'], 'L0_ffn_w1': _L0_ffn_in['w1'], 'L0_ffn_w2': _L0_ffn_in['w2'], 'L0_ffn_rms_w_s': _L0_ffn_in['rms_w_s'], 'L0_ffn_w1_s': _L0_ffn_in['w1_s'], 'L0_ffn_w2_s': _L0_ffn_in['w2_s'], 'L1_cond_W': _L1_cond_in['W'], 'L1_cond_b': _L1_cond_in['b'], 'L1_ffn_router_w': _L1_ffn_in['router_w'], 'L1_ffn_gate_w': _L1_ffn_in['gate_w'], 'L1_ffn_gate_b': _L1_ffn_in['gate_b'], 'L1_ffn_up_w': _L1_ffn_in['up_w'], 'L1_ffn_up_b': _L1_ffn_in['up_b'], 'L1_ffn_down_w': _L1_ffn_in['down_w'], 'L1_ffn_down_b': _L1_ffn_in['down_b']}

def reference(x, itok_B_0_2, itok_B_0_30, L0_cond_W1, L0_cond_b1, L0_cond_v, L0_ffn_router_w, L0_ffn_rms_w, L0_ffn_w1, L0_ffn_w2, L0_ffn_rms_w_s, L0_ffn_w1_s, L0_ffn_w2_s, L1_cond_W, L1_cond_b, L1_ffn_router_w, L1_ffn_gate_w, L1_ffn_gate_b, L1_ffn_up_w, L1_ffn_up_b, L1_ffn_down_w, L1_ffn_down_b):
    import jax
    import jax.numpy as jnp

    def _L0_cond_ref(hidden, W1, b1, v, prompt_type_ids):
        import jax, jax.numpy as jnp
        import numpy as np
        NEG_INF = -1e+30
        B, S, D = hidden.shape
        attn_in = jnp.tanh(jnp.einsum('bsd,da->bsa', hidden, W1) + b1)
        scores = jnp.einsum('bsa,a->bs', attn_in, v)
        idx = jnp.arange(S)
        j = idx[:, None]
        l = idx[None, :]
        prefix_m = l <= j
        postfix_m = l >= j
        cloze_m = l != j
        pt = prompt_type_ids[:, None, None]
        mask = jnp.where(pt == 0, prefix_m[None], jnp.where(pt == 1, postfix_m[None], cloze_m[None]))
        masked_scores = jnp.where(mask, scores[:, None, :], NEG_INF)
        p = jax.nn.softmax(masked_scores, axis=-1)
        cnt = jnp.sum(mask, axis=-1).astype(hidden.dtype)
        pooled = jnp.einsum('bjl,bld->bjd', p, hidden) / cnt[..., None]
        return pooled

    def _L0_ffn_ref(x, router_w, rms_w, w1, w2, rms_w_s, w1_s, w2_s):
        import jax, jax.numpy as jnp
        import numpy as np
        D_MODEL = 128
        HIDDEN = 256
        E_ROUTED = 14
        E_SHARED = 2
        TOP_K = 2
        EPS = 1e-09
        RMS_EPS = 1.1920929e-07

        def _ffn(xn, rw, W1, W2):
            ms = jnp.mean(xn * xn, axis=-1, keepdims=True)
            h = xn * jax.lax.rsqrt(ms + RMS_EPS) * rw
            return jax.nn.silu(h @ W1) @ W2
        B, T, D = x.shape
        N = B * T
        xf = x.reshape(N, D)
        gates = jax.nn.softmax(xf @ router_w, axis=-1)
        top_v, top_i = jax.lax.top_k(gates, TOP_K)
        masked = jnp.zeros_like(gates).at[jnp.arange(N)[:, None], top_i].set(top_v)
        masked = masked / (masked.sum(axis=-1, keepdims=True) + EPS)
        routed = jax.vmap(lambda rw_, W1_, W2_: _ffn(xf, rw_, W1_, W2_))(rms_w, w1, w2)
        routed_out = jnp.einsum('end,ne->nd', routed, masked)
        shared = jax.vmap(lambda rw_, W1_, W2_: _ffn(xf, rw_, W1_, W2_))(rms_w_s, w1_s, w2_s).sum(0)
        return (routed_out + shared).reshape(B, T, D)

    def _L1_cond_ref(x, cat_ids, W, b):
        import jax, jax.numpy as jnp
        import numpy as np
        C, I, O = (32, 128, 128)
        B, T = (64, 64)
        selected_W = W[cat_ids]
        selected_b = b[cat_ids]
        if x.ndim == 2:
            return jnp.einsum('bi,bio->bo', x, selected_W) + selected_b
        return jnp.einsum('bti,bio->bto', x, selected_W) + selected_b[:, None, :]

    def _L1_ffn_ref(x, router_w, gate_w, gate_b, up_w, up_b, down_w, down_b):
        import jax, jax.numpy as jnp
        import numpy as np
        D_MODEL, D_FF, N_EXPERTS, TOP_K = (128, 256, 8, 2)
        B, S = (2, 256)
        b, s, d = x.shape
        xf = x.reshape(b * s, d)
        n = xf.shape[0]
        router_logits = xf @ router_w.T
        probs = jax.nn.softmax(router_logits, axis=-1)
        topv, topi = jax.lax.top_k(probs, TOP_K)
        mask = jnp.zeros_like(probs).at[jnp.arange(n)[:, None], topi].set(1.0)
        probs = probs * mask
        probs = probs / (probs.sum(axis=-1, keepdims=True) + 1e-09)
        g = jnp.einsum('nd,edf->nef', xf, gate_w) + gate_b
        u = jnp.einsum('nd,edf->nef', xf, up_w) + up_b
        h = jax.nn.silu(g) * u
        expert_out = jnp.einsum('nef,efd->ned', h, down_w) + down_b
        y = jnp.einsum('ne,ned->nd', probs, expert_out)
        return y.reshape(b, s, d)
    x = x + _L0_ffn_ref(_L0_cond_ref(x, L0_cond_W1, L0_cond_b1, L0_cond_v, itok_B_0_2), L0_ffn_router_w, L0_ffn_rms_w, L0_ffn_w1, L0_ffn_w2, L0_ffn_rms_w_s, L0_ffn_w1_s, L0_ffn_w2_s)
    x = x + _L1_ffn_ref(_L1_cond_ref(x, itok_B_0_30, L1_cond_W, L1_cond_b), L1_ffn_router_w, L1_ffn_gate_w, L1_ffn_gate_b, L1_ffn_up_w, L1_ffn_up_b, L1_ffn_down_w, L1_ffn_down_b)
    return x

_drawn_inputs = setup_inputs


def setup_inputs(seed=0):
    import zlib

    import numpy as np

    out = dict(_drawn_inputs(seed))
    spreads = {'L0_ffn_rms_w': (1.0, 0.6),
     'L0_ffn_rms_w_s': (1.0, 0.6),
     'L1_cond_b': (0.0, 0.1),
     'L1_ffn_gate_b': (0.0, 0.8),
     'L1_ffn_up_b': (0.0, 0.8),
     'L1_ffn_down_b': (0.0, 0.1)}
    factors = {'L0_cond_b1': 31.975}
    for name, (base, spread) in spreads.items():
        noise = np.random.default_rng([zlib.crc32(name.encode()), seed]).standard_normal(out[name].shape)
        drawn = base * np.exp(spread * noise) if base else spread * noise
        out[name] = jnp.asarray(drawn.astype(out[name].dtype))
    for name, factor in factors.items():
        out[name] = (out[name] * factor).astype(out[name].dtype)
    return out
```

```python
from contextlib import ExitStack

import numpy as np

import concourse.bass as bass
from concourse import mybir

ALU = mybir.AluOpType
ACT = mybir.ActivationFunctionType
AX = mybir.AxisListType
F32 = mybir.dt.float32
F16 = mybir.dt.float16
BF16 = mybir.dt.bfloat16
I32 = mybir.dt.int32

P = 128
D = 128
B = 32
A = 32
F = 256
FC = F // P
ER, ES = 14, 2
E0 = ER + ES
E1 = 8
G = 2
NT = B // G
SLOTS = 256
HALVES = SLOTS // P
NEXP = (ER, E1)
TM = tuple(((NT * P * 2 + e * (SLOTS - 1)) // SLOTS + 1) // 2 * 2 for e in NEXP)
QB = 4
NQ = B // QB
WSCALE = 256.0
INV = 1.0 / WSCALE
BIG = 2.0 ** 100
LOW = -1e30
ICODE = 64.0

W1_HI, W1_LO = 0, F
W2_AT = 2 * F
REC0 = W2_AT + FC * 2 * D
G_HI, G_LO, U_HI, U_LO = 0, F, 2 * F, 3 * F
DN_AT = 4 * F
BIAS_AT = DN_AT + FC * 2 * D
DB_AT = BIAS_AT + 8
REC1 = DB_AT + D
WRING = 4
YRING = 4
RRING = 4

C_IDENT, C_USTRICT, C_DELTA = 0, 128, 256
C_CNT, C_IOTA, C_TILE, C_VMASK = 384, 387, 403, 435
NCONST = C_VMASK + 2 * 4 * B

CREDIT = 4


def constants():
    c = np.zeros((P, NCONST), np.float32)
    p = np.arange(P)
    c[:, C_IDENT:C_IDENT + P] = np.eye(P)
    c[:, C_USTRICT:C_USTRICT + P] = p[:, None] < p[None, :]
    c[:, C_DELTA:C_DELTA + P] = p[:, None] - p[None, :]
    c[:, C_CNT] = p + 1
    c[:, C_CNT + 1] = P - p
    c[:, C_CNT + 2] = P - 1
    c[:, C_IOTA:C_IOTA + 16] = np.arange(16) - ICODE
    c[:, C_TILE:C_TILE + 32] = np.arange(32)
    vm = c[:, C_VMASK:].reshape(P, 2, 4, B)
    for h in range(2):
        for bb in range(4):
            for g in range(4):
                vm[32 * g:32 * g + 32, h, bb, 16 * h + 4 * g + bb] = 1
    return c


def build(nc, x, ptype, cat, cw1, cb1, cv, rtr0, rms, w1, w2, rms_s, w1s, w2s, cW, cb,
          rtr1, gw, gb, uw, ub, dw, db, const, out):
    rows_d = [nc.dram_tensor(f"rows_{g}", [max(TM) * SLOTS, 2 * D], F16).ap() for g in range(G)]
    y_d = [nc.dram_tensor(f"expert_out_{g}", [max(TM) * SLOTS, D], F32).ap() for g in range(G)]

    with ExitStack() as ctx:
        def sb(name, shape, dt=F32):
            return ctx.enter_context(nc.sbuf_tensor(name, shape, dt))

        def sem(name):
            return ctx.enter_context(nc.semaphore(name))

        cst = sb("constants", [P, NCONST])
        ident, delta32 = cst[:, C_IDENT:C_IDENT + P], cst[:, C_DELTA:C_DELTA + P]
        ident16 = sb("ident16", [P, P], F16)
        ustrict16 = sb("ustrict16", [P, P], F16)
        ones16 = sb("ones16", [P, P], F16)
        identb = sb("identb", [P, P], BF16)
        deltab = sb("deltab", [P, P], BF16)
        scale_row = sb("scale_row", [1, P])
        xs = sb("x_rows", [P, B, D + 2])
        xT = sb("xT", [P, B * P])
        pooled = xT[:, :].rearrange("p (b d) -> p b d", b=B)
        hl = sb("rows_hl", [P, B, 2 * D], F16)
        hT = sb("hT", [P, 2, B * P], F16)
        cbrow = hT[0:1, :, :].rearrange("p a t -> p (a t)").bitcast(F32)
        rec0 = sb("records0", [P, E0, REC0], F16)
        rec1 = sb("records1", [P, E1, REC1], F16)
        wr = sb("record_ring", [P, WRING, REC1], F16)
        STG = 3 * F + 4 * D
        raw1 = wr[:, :, :].rearrange("p a c -> p (a c)")[:, 0:2 * 2 * STG].bitcast(F32).rearrange(
            "p (s c) -> p s c", s=2)
        wc = sb("cond_w", [P, B, 2 * D], F16)
        rowr = sb("row_ring", [P, RRING, HALVES, 2 * D], F16)
        xt = sb("xt", [P, 2, 2, SLOTS], F16)
        hf = sb("hidden32", [P, 2, 4 * SLOTS])
        hh = sb("hidden_hi", [P, 2, 4 * SLOTS], F16)
        hlo = sb("hidden_lo", [P, 2, 4 * SLOTS], F16)
        PT = hf[:, :, 0:QB * P]
        mk = hf[:, :, QB * P:2 * QB * P].bitcast(BF16).rearrange("p s (k c) -> p s k c", k=2)
        ys = sb("y_rows", [P, YRING, HALVES, D])
        gr = sb("gather_ring", [P, RRING, 2, D])
        raw0 = hh[:, :, :].bitcast(F32)
        attn = gr[:, :, :, :].rearrange("p (a s) k d -> p a (s k d)", a=2)
        mx = rowr[0:B, :, :, :].rearrange("p s h c -> p s (h c)").bitcast(F32)
        mrow = sb("row_max", [B, P])
        sT = sb("scores_t", [P, B])
        zeros = wc[:, :, :].rearrange("p b c -> p (b c)")[:, 0:max(TM) * SLOTS * 2 * D // P // 8]
        vrep = sb("v_rep", [P, 1])
        brep = sb("b1_rep", [P, 1])
        xt32 = xt[:, :, :, :].rearrange("p a k s -> p (a k s)").bitcast(F32)
        vsel = xt32[:, 0:2 * 4 * B]
        cw1s = sb("cond_w1", [P, A])
        ptc, ptb = sb("ptype_col", [B, 1], I32), sb("ptype_all", [P, B], I32)
        catr = sb("cat_row", [1, B], I32)
        selc = sb("sel_col", [B, 4])
        selb = sb("sel_all", [P, 4, B])
        cnt = sb("count", [P, B])
        rc = sb("pool_recip", [P, B])
        ssq = sb("sum_sq", [P, B])
        sq = sb("rms", [P, B])
        rr = sb("rms_recip", [P, B])
        squares_out = hlo[:, 1, :].bitcast(F32)
        vrows, ssb = xt32[0:56, 2 * P:3 * P], xt32[0:B, 3 * P:4 * P]
        vcols = sb("vector_cols", [P, 56])
        r0s, r0h = sb("router0", [P, ER]), sb("router0_hl", [P, 2, ER], F16)
        r1h = sb("router1_hl", [P, 2, E1], F16)
        dbr, dbh = sb("down_b", [E1, D]), sb("down_b_hl", [E1, 2, D], F16)
        lg, dd, d2 = sb("logits", [P, NT, 16]), sb("diff", [P, NT, 16]), sb("diff2", [P, NT, 16])
        ex, cd = sb("expd", [P, NT, 16]), sb("code", [P, NT, 16])
        oh1, oh2 = sb("onehot1", [P, NT, 16]), sb("onehot2", [P, NT, 16])
        oh16 = sb("onehot", [P, NT, 16], F16)
        sm = sb("small", [P, 12, NT])
        pre = sb("tile_prefix", [P, 2, 16 + NT, 16])
        nti, ntf = sb("tiles_int", [P, 2, 16], I32), sb("tiles", [P, 2, 32])
        cmp_ = sb("tile_cmp", [1, 32, 16])
        cmp_base = sb("first_slot", [P, 16])
        tef = sb("tile_expert_f", [1, 2, 32])
        te = sb("tile_expert", [1, 2, G, 32], I32)
        gwt = sb("gate_weights", [P, 2, 2, B])
        idx = sb("slot_index", [P, 2, 2, B], I32)
        xs16, xtt = (hh[:, 0, k * 4 * D:(k + 1) * 4 * D].rearrange("p (s c) -> p s c", s=2) for k in range(2))
        ctt = hh[:, 1, 0:4 * D].rearrange("p (s c) -> p s c", s=2)

        ps = ctx.enter_context(nc.psum_tensor("ps", [P, 8, 512], F32))

        def bank(n):
            return ps[:, n, :]

        def rank_bank(l):
            return bank(7 if l else 4)

        def bank16(n):
            return ps[:, n, :].bitcast(F16)

        s_const = sem("s_const"); s_small = sem("s_small"); s_x = [sem(f"s_xin{q}") for q in range(NQ)]
        s_zero = sem("s_zero"); s_zfill = sem("s_zfill"); s_pads = sem("s_pads"); s_tab = sem("s_tab")
        s_dve = sem("s_dve"); s_ms = sem("s_ms"); s_act = sem("s_act"); s_poolq = sem("s_poolq")
        s_raw0 = [sem(f"s_raw0_{i}") for i in range(2)]; s_rec0 = sem("s_rec0"); s_rec0hi = sem("s_rec0hi")
        s_raw1 = [sem(f"s_raw1_{i}") for i in range(2)]; s_rec1hi = sem("s_rec1hi"); s_rec1 = sem("s_rec1")
        s_vt = sem("s_vt"); s_vcols = sem("s_vcols"); s_db = sem("s_db"); s_dbrow = sem("s_dbrow")
        s_xTp = sem("s_xTp"); s_xT = sem("s_xT"); s_pa = sem("s_pa"); s_tanh = sem("s_tanh")
        s_vsel = sem("s_vsel"); s_sc = sem("s_sc"); s_ssb = sem("s_ssb"); s_sTp = sem("s_sTp"); s_sT = sem("s_sT")
        s_max = sem("s_max"); s_mk = sem("s_mk"); s_arg = sem("s_arg"); s_pt = sem("s_pt")
        s_pool = sem("s_pool"); s_pooled = sem("s_pooled"); s_ssq = sem("s_ssq"); s_sqrt = sem("s_sqrt")
        s_h0 = sem("s_h0"); s_hhi = sem("s_hhi"); s_hlo = sem("s_hlo"); s_hTp = sem("s_hTp"); s_hT = sem("s_hT")
        s_lg = [sem("s_lg0"), sem("s_lg1")]; s_diff = [sem("s_diff0"), sem("s_diff1")]
        s_ex = [sem("s_ex0"), sem("s_ex1")]; s_oh = [sem("s_oh0"), sem("s_oh1")]
        s_rank = [sem("s_rank0"), sem("s_rank1")]; s_idx = [sem("s_idx0"), sem("s_idx1")]
        s_scat = [[sem(f"s_scat{l}_{g}") for g in range(G)] for l in range(2)]
        s_sU = sem("s_sU"); s_sS = sem("s_sS"); s_sHi = sem("s_sHi"); s_sLo = sem("s_sLo")
        s_sD = sem("s_sD"); s_sY = sem("s_sY")
        L = [dict(rows=[sem(f"l{l}_rows{i}") for i in range(RRING // 2)],
                  w=[sem(f"l{l}_w{i}") for i in range(WRING)],
                  st=[sem(f"l{l}_store{i}") for i in range(YRING // 2)],
                  **{k: sem(f"l{l}_{k}") for k in ("T", "xt", "U", "silu", "h", "hi", "lo", "D", "y")})
             for l in range(2)]
        s_gr = [sem(f"s_gather{i}") for i in range(RRING)]
        s_x1 = sem("s_x1"); s_xhi = sem("s_xhi"); s_xlo = sem("s_xlo"); s_t2 = sem("s_t2"); s_xtt = sem("s_xtt")
        s_c = sem("s_c"); s_chi = sem("s_chi"); s_clo = sem("s_clo"); s_t3 = sem("s_t3"); s_ctt = sem("s_ctt")
        s_cb = sem("s_cb"); s_out = sem("s_out"); s_credit = sem("s_credit")

        def done(n):
            return n + 1 + CREDIT

        block = ctx.enter_context(nc.Block())

        @block.sync
        def _(sp):
            sp.dma_start(cst[:, :], const).then_inc(s_const, 16)
            for q in range(2):
                sp.dma_start(xs[:, QB * q:QB * q + QB, 0:D],
                             x[QB * q:QB * q + QB].rearrange("b p d -> p b d")).then_inc(s_x[q], 16)
            sp.dma_start(cw1s[:, :], cw1).then_inc(s_small, 16)
            for g in range(4):
                sp.dma_start(brep[32 * g:32 * g + 32, :], cb1.rearrange("(a o) -> a o", o=1)).then_inc(s_small, 16)
                sp.dma_start(vrep[32 * g:32 * g + 32, :], cv.rearrange("(a o) -> a o", o=1)).then_inc(s_small, 16)
            for q in range(2, NQ):
                sp.dma_start(xs[:, QB * q:QB * q + QB, 0:D],
                             x[QB * q:QB * q + QB].rearrange("b p d -> p b d")).then_inc(s_x[q], 16)
            sp.dma_start(ptc[:, :], ptype.rearrange("(a o) -> a o", o=1)).then_inc(s_small, 16)
            sp.dma_start(ptb[:, :], ptype.rearrange("(o a) -> o a", o=1).broadcast_to([P, B])).then_inc(s_small, 16)
            sp.dma_start(catr[:, :], cat.rearrange("(o a) -> o a", o=1)).then_inc(s_small, 16)
            sp.dma_start(vrows[0:14, :], rms).then_inc(s_small, 16)
            sp.dma_start(vrows[14:16, :], rms_s).then_inc(s_small, 16)
            sp.dma_start(vrows[16:32, :], gb.rearrange("e (c p) -> (e c) p", p=P)).then_inc(s_small, 16)
            sp.dma_start(vrows[32:48, :], ub.rearrange("e (c p) -> (e c) p", p=P)).then_inc(s_small, 16)
            sp.dma_start(vrows[48:56, :], rtr1).then_inc(s_small, 16)
            sp.dma_start(r0s[:, :], rtr0).then_inc(s_small, 16)
            sp.dma_start(dbr[:, :], db).then_inc(s_small, 16)
            for e in range(E0):
                if e >= 2:
                    sp.wait_ge(s_rec0, e - 1)
                a, b_ = (w1[e], w2[e]) if e < ER else (w1s[e - ER], w2s[e - ER])
                sp.dma_start(raw0[:, e % 2, 0:F], a).then_inc(s_raw0[e % 2], 16)
                sp.dma_start(raw0[:, e % 2, F:2 * F].rearrange("p (c n) -> p c n", c=FC),
                             b_.rearrange("(c p) n -> p c n", p=P)).then_inc(s_raw0[e % 2], 16)
                if e == 1:
                    sp.wait_ge(s_zero, 1)
                    for g in range(G):
                        n = zeros.shape[1]
                        sp.dma_start(rows_d[g].rearrange("(p r) c -> p (r c)", p=P).rearrange("p (k n) -> p k n", n=n),
                                     zeros[:, :].unsqueeze(1).broadcast_to([P, 8, n])).then_inc(s_zfill, 16)
            sp.wait_ge(s_db, 2)
            sp.dma_start(rec1[0:1, :, DB_AT:DB_AT + D], dbh[:, 0, :]).then_inc(s_dbrow, 16)
            sp.dma_start(rec1[1:2, :, DB_AT:DB_AT + D], dbh[:, 1, :]).then_inc(s_dbrow, 16)
            for e in range(E1):
                if e >= 2:
                    sp.wait_ge(s_rec1, e - 1)
                for k, w in enumerate((gw, uw)):
                    sp.dma_start(raw1[:, e % 2, k * F:k * F + F], w[e]).then_inc(s_raw1[e % 2], 16)
                sp.dma_start(raw1[:, e % 2, 2 * F:3 * F].rearrange("p (c n) -> p c n", c=FC),
                             dw[e].rearrange("(c p) n -> p c n", p=P)).then_inc(s_raw1[e % 2], 16)
                if e == 0:
                    sp.wait_ge(s_small, 16 * 19)
                for j in range(4):
                    b = 4 * e + j
                    c = sp.value_load(catr[0:1, b:b + 1], min_val=0, max_val=cW.shape[0] - 1)
                    sp.dma_start(raw1[:, e % 2, 3 * F + j * D:3 * F + j * D + D],
                                 cW[bass.ds(c, 1), :, :].rearrange("a p d -> (a p) d")).then_inc(s_raw1[e % 2], 16)

            def tile_loads(l, g):
                rec, nrec, s = (rec0, REC0, L[0]) if l == 0 else (rec1, REC1, L[1])
                src2 = rows_d[g].rearrange("(t h p) c -> t p h c", h=2 * HALVES, p=P)
                base, tm = g * TM[l], TM[l]

                def load_rows(i, j):
                    off = WRING * i if type(i) is not int else 0
                    pair = (base + j) // 2 % (RRING // 2)
                    sp.wait_ge(s["T"], base + j + 2 + off)
                    sp.dma_start(rowr[:, 2 * pair:2 * pair + 2, :, :].rearrange("p t h c -> p (t h) c"),
                                 src2[bass.ds(j // 2 + (WRING // 2 * i if type(i) is not int else 0), 1)].rearrange(
                                     "a p h c -> (a p) h c")).then_inc(s["rows"][pair], 16)

                def load_record(i, j):
                    off = WRING * i if type(i) is not int else 0
                    slot = (base + j) % WRING
                    e = sp.value_load(te[0:1, l, g, bass.ds(j + off, 1)], min_val=0, max_val=NEXP[l] - 1)
                    sp.wait_ge(s["D"], base + j + 1 + off)
                    sp.dma_start(wr[:, slot, 0:nrec].bitcast(I32),
                                 rec[:, bass.ds(e, 1), :].rearrange("p a c -> p (a c)").bitcast(I32)).then_inc(
                                     s["w"][slot], 16)
                sp.wait_ge(s_idx[l], g + 1)
                sp.wait_ge(s_scat[l][g], 16 * 2 * NT)
                load_rows(0, 0)
                loops = (tm - 2) // WRING
                with sp.Fori(0, loops) as turn:
                    for j in range(0, WRING, 2):
                        load_rows(turn, j + 2)
                        load_record(turn, j)
                        load_record(turn, j + 1)
                for j in range(WRING * loops, tm, 2):
                    if j + 2 < tm:
                        load_rows(0, j + 2)
                    load_record(0, j)
                    load_record(0, j + 1)

            sp.wait_ge(s_rec1, E1)
            sp.wait_ge(s_dbrow, 32)
            sp.wait_ge(s_credit, 1)
            for g in range(G):
                tile_loads(0, g)
            sp.wait_ge(s_sU, 2 * NQ)
            for b in range(B):
                c = sp.value_load(catr[0:1, b:b + 1], min_val=0, max_val=cb.shape[0] - 1)
                sp.dma_start(cbrow[0:1, b * D:b * D + D], cb[bass.ds(c, 1), :]).then_inc(s_cb, 16)
            for g in range(G):
                tile_loads(1, g)
            for q in range(NQ):
                sp.wait_ge(s_x1, B + QB * (q + 1))
                sp.dma_start(out[QB * q:QB * q + QB].rearrange("b p d -> p b d"),
                             xs[:, QB * q:QB * q + QB, 0:D]).then_inc(s_out, 16)
            sp.wait_ge(s_out, 16 * NQ)

        @block.gpsimd
        def _(pool):
            nc.gpsimd.memset(zeros[:, :], 0.0).then_inc(s_zero, 1)
            nc.gpsimd.memset(mx[:, :, :], LOW).then_inc(s_pads, 1)
            nc.gpsimd.memset(xs[:, :, D:D + 2], 1.0).then_inc(s_pads, 1)
            nc.gpsimd.memset(pre[:, :, :, :], 0.0).then_inc(s_pads, 1)
            nc.gpsimd.memset(ntf[:, :, :], 0.0).then_inc(s_pads, 1)
            nc.gpsimd.memset(rec1[:, :, DB_AT:DB_AT + D], 0.0).then_inc(s_pads, 1)
            nc.gpsimd.memset(scale_row[:, :], WSCALE).then_inc(s_pads, 1)
            nc.gpsimd.memset(ones16[:, :], 1.0).then_inc(s_pads, 1)
            def scatter(l, g):
                if l == 0:
                    pool.wait_ge(s_zfill, 16 * G)
                    pool.wait_ge(s_hlo, (g + 1) * NT // QB)
                else:
                    pool.wait_ge(s_clo, (g + 1) * NT)
                    for k in range(RRING // 2):
                        pool.wait_ge(L[0]["rows"][k], 16 * len(
                            [t for t in range(0, (g + 1) * TM[0], 2) if t // 2 % (RRING // 2) == k]))
                pool.wait_ge(s_idx[l], g + 1)
                for t in range(NT):
                    b = g * NT + t
                    for k in range(2):
                        nc.gpsimd.indirect_dma_start(
                            rows_d[g], bass.IndirectOffsetOnAxis(ap=idx[:, l, k, b:b + 1], axis=0),
                            hl[:, b, :], None).then_inc(s_scat[l][g], 16)

            def gather(l, g):
                for k in range(2):
                    stored = len([t for t in range(0, (g + 1) * TM[l], 2) if t // 2 % 2 == k])
                    pool.wait_ge(L[l]["st"][k], 16 * (stored + 1))
                for t in range(NT):
                    b = g * NT + t
                    n = l * B + b
                    if n >= RRING:
                        pool.wait_ge(s_x1, n - RRING + 1)
                    for k in range(2):
                        nc.gpsimd.indirect_dma_start(
                            gr[:, n % RRING, k, :], None, y_d[g],
                            bass.IndirectOffsetOnAxis(ap=idx[:, l, k, b:b + 1], axis=0)).then_inc(s_gr[n % RRING], 16)

            for s in L:
                for k in ("T", "xt", "U", "silu", "h", "hi", "lo", "D", "y"):
                    pool.sem_inc(s[k], CREDIT)
                for k in range(2):
                    pool.sem_inc(s["st"][k], 16)
            pool.sem_inc(s_credit, 1)
            for g in range(G):
                scatter(0, g)
            for g in range(G):
                gather(0, g)
                if g > 0:
                    scatter(1, g - 1)
            scatter(1, G - 1)
            for g in range(G):
                gather(1, g)

        @block.tensor
        def _(pe):
            pe.wait_ge(s_const, 16)
            pe.wait_ge(s_small, 16 * 19)
            pe.transpose(bank(5)[:, 0:56], vrows[:, :], ident[0:56, 0:56]).then_inc(s_vt, 1)
            for q in range(NQ + 1):
                if q < NQ:
                    pe.wait_ge(s_x[q], 16)
                    if q >= 2:
                        pe.wait_ge(s_xT, q - 1)
                    for j in range(QB):
                        mm = pe.transpose(bank(q % 2)[:, j * P:j * P + P], xs[:, QB * q + j, 0:D], ident)
                    mm.then_inc(s_xTp, 1)
                if q >= 1:
                    k = q - 1
                    pe.wait_ge(s_xT, k + 1)
                    h, g = k // 4, k % 4
                    mm = pe.matmul(ps[32 * g:32 * g + 32, 2 + h, :], cw1s[:, :],
                                   xT[:, k * QB * P:(k + 1) * QB * P], start=True, stop=True)
                    if g == 3:
                        mm.then_inc(s_pa, 1)
            pe.wait_ge(s_vsel, 1)
            for h in range(2):
                pe.wait_ge(s_tanh, h + 1)
                for bb in range(4):
                    mm = pe.matmul(bank(4)[0:B, 0:P], vsel[:, (4 * h + bb) * B:(4 * h + bb + 1) * B],
                                   attn[:, h, bb * P:bb * P + P], start=(h + bb == 0), stop=(h + bb == 4))
            mm.then_inc(s_sc, 1)
            pe.wait_ge(s_ssb, 1)
            pe.wait_ge(s_vcols, 1)
            pe.transpose(bank(5)[:, 0:B], ssb[:, :], ident[0:B, 0:B]).then_inc(s_sTp, 1)
            pe.wait_ge(s_max, 1)

            def exponent(q):
                pe.wait_ge(s_mk, q + 1)
                if q >= 2:
                    pe.wait_ge(s_pt, q - 1)
                o = bank(6 + q % 2)
                for j in range(QB):
                    b = QB * q + j
                    pe.matmul(o[:, j * P:j * P + P], ident[0:B, b:b + 1].broadcast_to([B, P]), mrow[:, :],
                              start=(j == 0), stop=False, skip_group_check=True)
                pe.matmul(o, identb[:, :], mk[:, q % 2, 0, :], start=False, stop=False, skip_group_check=True)
                mm = pe.matmul(o, identb[:, :], mk[:, q % 2, 1, :], start=False, stop=True, skip_group_check=True)
                mm.then_inc(s_arg, 1)

            def pool_mm(q):
                pe.wait_ge(s_pt, q + 1)
                if q >= 2:
                    pe.wait_ge(s_pooled, q - 1)
                for j in range(QB):
                    mm = pe.matmul(ps[:, 2 * (q % 2) + j // 2, 256 * (j % 2):256 * (j % 2) + D + 1],
                                   PT[:, q % 2, j * P:j * P + P], xs[:, QB * q + j, 0:D + 1], start=True, stop=True)
                mm.then_inc(s_pool, 1)

            def rank_mm(l, g):
                pe.wait_ge(s_oh[l], g + 1)
                n, e = NT * NEXP[l], NEXP[l]
                o = oh16[:, :, 0:e]
                pe.matmul(rank_bank(l)[:, 0:n], ustrict16[:, :], o, start=True, stop=True)
                pe.matmul(rank_bank(l)[:, 256:256 + n], ones16[:, :], o, start=True, stop=True).then_inc(s_rank[l], 1)

            for g in range(G):
                q0, q1 = g * NQ // G, (g + 1) * NQ // G
                exponent(q0)
                for q in range(q0, q1):
                    if q + 1 < q1:
                        exponent(q + 1)
                    pool_mm(q)
                for q in range(q0, q1):
                    pe.wait_ge(s_hlo, q + 1)
                    if q >= 1:
                        pe.wait_ge(s_hT, q)
                    if g >= 1 and q == q0:
                        pe.wait_ge(s_idx[0], g)
                    for k in range(2):
                        for j in range(QB):
                            mm = pe.transpose(bank16(4)[:, (k * QB + j) * P:(k * QB + j + 1) * P],
                                              hl[:, QB * q + j, k * D:k * D + D], ident16[:, :])
                    mm.then_inc(s_hTp, 1)
                for q in range(q0, q1):
                    pe.wait_ge(s_hT, q + 1)
                    if g >= 1 and q == q0:
                        pe.wait_ge(s_idx[0], g)
                    for j in range(QB):
                        b = QB * q + j
                        o = bank(5)[:, (b - g * NT) * ER:(b - g * NT + 1) * ER]
                        th, tl = hT[:, 0, b * P:b * P + P], hT[:, 1, b * P:b * P + P]
                        pe.matmul(o, th, r0h[:, 0, :], start=True, stop=False, skip_group_check=True)
                        pe.matmul(o, th, r0h[:, 1, :], start=False, stop=False, skip_group_check=True)
                        mm = pe.matmul(o, tl, r0h[:, 0, :], start=False, stop=True, skip_group_check=True)
                mm.then_inc(s_lg[0], 1)
                rank_mm(0, g)

            def shared_up(k, j):
                n = 2 * k + j
                if n >= 2:
                    pe.wait_ge(s_sS, n - 1)
                e = ER + j
                for c in range(FC):
                    o = bank(2 + 2 * j + c)
                    wh = rec0[:, e, W1_HI + c * P:W1_HI + c * P + P]
                    wl = rec0[:, e, W1_LO + c * P:W1_LO + c * P + P]
                    th = hT[:, 0, k * 512:(k + 1) * 512]
                    tl = hT[:, 1, k * 512:(k + 1) * 512]
                    pe.matmul(o, wh, th, start=True, stop=False)
                    pe.matmul(o, wh, tl, start=False, stop=False)
                    mm = pe.matmul(o, wl, th, start=False, stop=True)
                mm.then_inc(s_sU, 1)

            def shared_down(k):
                pe.wait_ge(s_sLo, 2 * k + 2)
                if k >= 2:
                    pe.wait_ge(s_sY, k - 1)
                for t in range(QB):
                    o = bank(6 + k % 2)[:, t * D:t * D + D]
                    first = True
                    for j in range(ES):
                        for c in range(FC):
                            at = W2_AT + 2 * D * c
                            w2h, w2l = rec0[:, ER + j, at:at + D], rec0[:, ER + j, at + D:at + 2 * D]
                            h_, l_ = (v[:, j, c * 512 + t * P:c * 512 + t * P + P] for v in (hh, hlo))
                            pe.matmul(o, h_, w2h, start=first, stop=False, skip_group_check=True)
                            pe.matmul(o, h_, w2l, start=False, stop=False, skip_group_check=True)
                            mm = pe.matmul(o, l_, w2h, start=False, stop=(j == ES - 1 and c == FC - 1),
                                           skip_group_check=True)
                            first = False
                mm.then_inc(s_sD, 1)

            pe.wait_ge(s_rec0, E0)
            pe.wait_ge(s_pooled, NQ)
            pe.wait_ge(s_idx[0], G)
            for k in range(NQ + 1):
                if k < NQ:
                    for j in range(ES):
                        shared_up(k, j)
                if k >= 1:
                    shared_down(k - 1)

            def tile_T(l, n, slot, b):
                s = L[l]
                pe.wait_ge(s["rows"][slot // 2], 16 * (n_turn(n) + 1))
                pe.wait_ge(s["xt"], val(n) + 3)
                for k in range(2):
                    for h in range(HALVES):
                        mm = pe.transpose(bank16(b)[:, (k * HALVES + h) * P:(k * HALVES + h + 1) * P],
                                          rowr[:, slot, h, k * D:k * D + D], ident16[:, :])
                mm.then_inc(s["T"], 1)

            def val(n):
                return n[0]

            def n_turn(n):
                return n[1]

            def tile_U(l, n, slot, b):
                s = L[l]
                pe.wait_ge(s["xt"], val(n) + 1 + CREDIT)
                pe.wait_ge(s["w"][slot], 16 * (n_turn(n) + 1))
                pe.wait_ge(s["silu" if l == 0 else "h"], val(n) + 3)
                for m in range(1 + l):
                    for c in range(FC):
                        o = bank(2 + 2 * b + m)[:, c * SLOTS:(c + 1) * SLOTS]
                        at = 2 * F * m + c * P
                        wh, wl = wr[:, slot, at:at + P], wr[:, slot, at + F:at + F + P]
                        pe.matmul(o, wh, xt[:, b, 0, :], start=True, stop=False, skip_group_check=True)
                        pe.matmul(o, wh, xt[:, b, 1, :], start=False, stop=False, skip_group_check=True)
                        mm = pe.matmul(o, wl, xt[:, b, 0, :], start=False, stop=True, skip_group_check=True)
                mm.then_inc(s["U"], 1)

            def tile_D(l, n, slot, b):
                s = L[l]
                pe.wait_ge(s["lo"], val(n) + 1 + CREDIT)
                pe.wait_ge(s["y"], val(n) + 3)
                at0 = W2_AT if l == 0 else DN_AT
                for h in range(HALVES):
                    o = bank(6 + b)[:, h * D:h * D + D]
                    for c in range(FC):
                        at = at0 + 2 * D * c
                        w2h, w2l = wr[:, slot, at:at + D], wr[:, slot, at + D:at + 2 * D]
                        f = c * SLOTS + h * P
                        pe.matmul(o, hh[:, b, f:f + P], w2h, start=(c == 0), stop=False, skip_group_check=True)
                        pe.matmul(o, hh[:, b, f:f + P], w2l, start=False, stop=False, skip_group_check=True)
                        mm = pe.matmul(o, hlo[:, b, f:f + P], w2h, start=False,
                                       stop=(c == FC - 1 and l == 0), skip_group_check=True)
                    if l == 1:
                        mm = pe.matmul(o, ones16[:, :], wr[:, slot, DB_AT:DB_AT + D], start=False, stop=True,
                                       skip_group_check=True)
                mm.then_inc(s["D"], 1)

            def tiles(l, g):
                base, tm = g * TM[l], TM[l]

                def num(i):
                    return (base + i, (base + i) // WRING), (base + i) % WRING, (base + i) % 2

                def step(i):
                    if i + 1 < tm:
                        n, slot, b = num(i + 1)
                        tile_T(l, n, slot, b)
                    if 0 <= i < tm:
                        n, slot, b = num(i)
                        tile_U(l, n, slot, b)
                    if i >= 1:
                        n, slot, b = num(i - 1)
                        tile_D(l, n, slot, b)
                step(-1)
                step(0)
                loops = (tm - 2) // WRING
                with pe.Fori(0, loops) as turn:
                    for j in range(WRING):
                        def at(d):
                            k = base + 1 + j + d
                            return (WRING * turn + k, turn + k // WRING), k % WRING, k % 2
                        tile_T(l, *at(1))
                        tile_U(l, *at(0))
                        tile_D(l, *at(-1))
                for i in range(1 + loops * WRING, tm + 1):
                    step(i)

            pe.wait_ge(s_sY, NQ)
            for g in range(G):
                tiles(0, g)
            pe.wait_ge(s_cb, 16 * B)
            for k in ("y",):
                pe.wait_ge(L[0][k], G * TM[0] + CREDIT)

            def front1(g):
                for t in range(NT + 3):
                    if t < NT:
                        b = n = g * NT + t
                        pe.wait_ge(s_xlo, n + 1)
                        if n >= 2:
                            pe.wait_ge(s_xtt, n - 1)
                        for k in range(2):
                            mm = pe.transpose(bank16(n % 2)[:, k * P:k * P + P], xs16[:, n % 2, k * D:k * D + D],
                                              ident16[:, :])
                        mm.then_inc(s_t2, 1)
                    if 0 <= t - 1 < NT:
                        b = n = g * NT + t - 1
                        pe.wait_ge(s_xtt, n + 1)
                        if n >= 2:
                            pe.wait_ge(s_clo, n - 1)
                        o = bank(2 + n % 2)[:, 0:D]
                        pe.matmul(o, xtt[:, n % 2, 0:P], wc[:, b, 0:D], start=True, stop=False)
                        pe.matmul(o, xtt[:, n % 2, 0:P], wc[:, b, D:2 * D], start=False, stop=False)
                        pe.matmul(o, xtt[:, n % 2, P:2 * P], wc[:, b, 0:D], start=False, stop=False)
                        pe.matmul(o, scale_row[:, :], cbrow[0:1, b * D:b * D + D], start=False,
                                  stop=True).then_inc(s_c, 1)
                    if 0 <= t - 2 < NT:
                        b = n = g * NT + t - 2
                        pe.wait_ge(s_clo, n + 1)
                        if n >= 2:
                            pe.wait_ge(s_ctt, n - 1)
                        for k in range(2):
                            mm = pe.transpose(bank16(4 + n % 2)[:, k * P:k * P + P], hl[:, b, k * D:k * D + D],
                                              ident16[:, :])
                        mm.then_inc(s_t3, 1)
                    if 0 <= t - 3 < NT:
                        b = n = g * NT + t - 3
                        pe.wait_ge(s_ctt, n + 1)
                        if g >= 1 and t == 3:
                            pe.wait_ge(s_idx[1], g)
                        o = bank(6)[:, (t - 3) * E1:(t - 2) * E1]
                        pe.matmul(o, ctt[:, n % 2, 0:P], r1h[:, 0, :], start=True, stop=False, skip_group_check=True)
                        pe.matmul(o, ctt[:, n % 2, 0:P], r1h[:, 1, :], start=False, stop=False, skip_group_check=True)
                        mm = pe.matmul(o, ctt[:, n % 2, P:2 * P], r1h[:, 0, :], start=False, stop=True,
                                       skip_group_check=True)
                        mm.then_inc(s_lg[1], 1)
                rank_mm(1, g)

            for g in range(G):
                front1(g)
            pe.wait_ge(s_idx[1], G)
            for g in range(G):
                tiles(1, g)

        @block.scalar
        def _(act):
            chain = [0]

            def link(ins):
                chain[0] += 1
                ins.then_inc(s_act, 1)
                act.wait_ge(s_act, chain[0])

            def copy_xT(q):
                act.wait_ge(s_xTp, q + 1)
                nc.scalar.copy(xT[:, q * QB * P:(q + 1) * QB * P], bank(q % 2)).then_inc(s_xT, 1)

            def route_act(l, g):
                e = NEXP[l]
                act.wait_ge(s_diff[l], g + 1)
                nc.scalar.activation(ex[:, :, 0:e], dd[:, :, 0:e], ACT.Exp, scale=INV)
                nc.scalar.activation(sm[:, 1, :], sm[:, 0, :], ACT.Exp, scale=INV).then_inc(s_ex[l], 1)

            for q in range(NQ):
                copy_xT(q)
            act.wait_ge(s_small, 16 * 19)
            for h in range(2):
                act.wait_ge(s_pa, h + 1)
                nc.scalar.activation(attn[:, h, :], bank(2 + h), ACT.Tanh, bias=brep[:, 0:1]).then_inc(s_tanh, 1)

            def split0(e):
                if e == 0:
                    act.wait_ge(s_vcols, 2)
                act.wait_ge(s_raw0[e % 2], 32 * (e // 2 + 1))
                nc.scalar.mul(rec0[:, e, W1_HI:W1_HI + F], raw0[:, e % 2, 0:F], vcols[:, e:e + 1])
                nc.scalar.mul(rec0[:, e, W2_AT:REC0].rearrange("p (c k n) -> p c k n", c=FC, k=2)[:, :, 0, :],
                              raw0[:, e % 2, F:2 * F].rearrange("p (c n) -> p c n", c=FC), WSCALE).then_inc(s_rec0hi, 1)

            act.wait_ge(s_sT, 1)
            for g in range(G):
                q0, q1 = g * NQ // G, (g + 1) * NQ // G

                def squares(q):
                    act.wait_ge(s_pooled, q + 1)
                    if q >= 1:
                        act.wait_ge(s_ssq, q)
                    for j in range(QB):
                        b = QB * q + j
                        ins = nc.scalar.activation(squares_out[:, j * D:j * D + D], pooled[:, b, :], ACT.Square,
                                                   accum_out=ssq[:, b:b + 1])
                    ins.then_inc(s_ssq, 1)
                for q in range(q0, q1):
                    act.wait_ge(s_arg, q + 1)
                    if q >= 2:
                        act.wait_ge(s_pool, q - 1)
                    for j in range(QB):
                        b = QB * q + j
                        ins = nc.scalar.activation(PT[:, q % 2, j * P:j * P + P], bank(6 + q % 2)[:, j * P:j * P + P],
                                                   ACT.Exp, bias=sT[:, b:b + 1], scale=-1.0)
                    ins.then_inc(s_pt, 1)
                    split0(2 * q)
                    split0(2 * q + 1)
                    if q > q0:
                        squares(q - 1)
                squares(q1 - 1)
                gs = slice(g * NT, (g + 1) * NT)
                act.wait_ge(s_ms, g + 1)
                nc.scalar.activation(sq[:, gs], rr[:, gs], ACT.Sqrt).then_inc(s_sqrt, 1)
                for q in range(q0, q1):
                    act.wait_ge(s_h0, q + 1)
                    nc.scalar.copy(hl[:, QB * q:QB * q + QB, 0:D], pooled[:, QB * q:QB * q + QB, :]).then_inc(s_hhi, 1)
                route_act(0, g)

            def shared_silu(n):
                act.wait_ge(s_sU, n + 1)
                if n >= 2:
                    act.wait_ge(s_sLo, n - 1)
                j = n % 2
                nc.scalar.activation(hf[:, j, :].rearrange("p (c t) -> p c t", c=FC), ps[:, 2 + 2 * j:4 + 2 * j, :],
                                     ACT.Silu, scale=INV).then_inc(s_sS, 1)

            def split_w(e):
                act.wait_ge(s_raw1[e % 2], 16 * 7 * (e // 2 + 1))
                r = raw1[:, e % 2, :]
                nc.scalar.mul(rec1[:, e, 0:4 * F].rearrange("p (m k f) -> p m k f", m=2, k=2)[:, :, 0, :],
                              r[:, 0:2 * F].rearrange("p (m f) -> p m f", m=2), WSCALE)
                nc.scalar.mul(rec1[:, e, DN_AT:BIAS_AT].rearrange("p (c k n) -> p c k n", c=FC, k=2)[:, :, 0, :],
                              r[:, 2 * F:3 * F].rearrange("p (c n) -> p c n", c=FC), WSCALE)
                nc.scalar.mul(wc[:, 4 * e:4 * e + 4, 0:D], r[:, 3 * F:].rearrange("p (b n) -> p b n", b=4),
                              WSCALE).then_inc(s_rec1hi, 1)

            nc.scalar.preload_act_table(ACT.Silu)
            act.wait_ge(s_zfill, 16 * G)
            for k in range(NQ):
                shared_silu(2 * k)
                split_w(k)
                shared_silu(2 * k + 1)

            def tiles(l, g):
                s = L[l]
                base, tm = g * TM[l], TM[l]

                def copy_x(n, b):
                    act.wait_ge(s["T"], n + 1 + CREDIT)
                    act.wait_ge(s["U"], n + 3)
                    nc.scalar.copy(xt[:, b, :, :].rearrange("p k s -> p (k s)"),
                                   bank16(b)[:, 0:2 * SLOTS]).then_inc(s["xt"], 1)

                def silu(n, b):
                    act.wait_ge(s["U"], n + 1 + CREDIT)
                    act.wait_ge(s["lo"], n + 3)
                    if l == 0:
                        nc.scalar.activation(hf[:, b, 0:FC * SLOTS], bank(2 + 2 * b), ACT.Silu,
                                             scale=INV).then_inc(s["silu"], 1)
                    else:
                        slot = None
                        for c in range(FC):
                            ins = nc.scalar.activation(hf[:, b, (2 + c) * SLOTS:(3 + c) * SLOTS],
                                                       bank(2 + 2 * b)[:, c * SLOTS:(c + 1) * SLOTS], ACT.Silu,
                                                       bias=bias_of(b_slot[0], c), scale=INV)
                        ins.then_inc(s["silu"], 1)

                b_slot = [0]

                def y_copy(n, k, turn):
                    act.wait_ge(s["D"], n + 1 + CREDIT)
                    if k % 2 == 0:
                        act.wait_ge(s["st"][k // 2 % 2], 16 * (k // 4 + turn + 1))
                    nc.scalar.copy(ys[:, k % YRING, :, :].rearrange("p h d -> p (h d)"),
                                   bank(6 + k % 2)[:, 0:HALVES * D]).then_inc(s["y"], 1)

                def store(i, n, k):
                    act.wait_ge(s["y"], n + 1 + CREDIT)
                    pair = k // 2 % (YRING // 2)
                    act.dma_start(y_d[g].rearrange("(t h p) d -> t p h d", h=2 * HALVES, p=P)[bass.ds(i, 1)].rearrange(
                        "a p h d -> (a p) h d"),
                        ys[:, 2 * pair:2 * pair + 2, :, :].rearrange("p t h d -> p (t h) d")).then_inc(s["st"][pair], 16)

                def step(i0, k0, turn):
                    off = WRING * turn if type(turn) is not int else 0
                    ok = (lambda d: True) if type(turn) is not int else (lambda d: 0 <= i0 + d < tm)
                    if ok(1):
                        n = base + i0 + 1
                        copy_x(n + off, n % 2)
                    if ok(0):
                        n = base + i0
                        b_slot[0] = n % WRING
                        silu(n + off, n % 2)
                    if ok(-1):
                        n = base + i0 - 1
                        if l == 1:
                            y_copy(n + off, n, turn)
                        if n % 2 == 1:
                            store((i0 - 2) // 2 + (WRING // 2 * turn if type(turn) is not int else 0), n + off, n)
                step(-1, 0, 0)
                step(0, 0, 0)
                loops = (tm - 2) // WRING
                with act.Fori(0, loops) as turn:
                    for j in range(WRING):
                        step(1 + j, 0, turn)
                for i in range(1 + loops * WRING, tm + 1):
                    step(i, 0, 0)

            def bias_of(slot, k):
                return wr[:, slot, BIAS_AT + 2 * k:BIAS_AT + 2 * k + 2].bitcast(F32)

            for g in range(G):
                tiles(0, g)

            def front1(g):
                for t in range(NT + 1):
                    if t < NT:
                        b = n = g * NT + t
                        act.wait_ge(s_x1, n + 1)
                        if n >= 2:
                            act.wait_ge(s_t2, n - 1)
                        nc.scalar.copy(xs16[:, n % 2, 0:D], xs[:, b, 0:D]).then_inc(s_xhi, 1)
                        act.wait_ge(s_t2, n + 1)
                        if n >= 2:
                            act.wait_ge(s_c, n - 1)
                        nc.scalar.copy(xtt[:, n % 2, :], bank16(n % 2)[:, 0:2 * P]).then_inc(s_xtt, 1)
                    if t >= 1:
                        b = n = g * NT + t - 1
                        act.wait_ge(s_c, n + 1)
                        if t == 1:
                            act.wait_ge(s_scat[0][g], 16 * 2 * NT)
                        nc.scalar.mul(hl[:, b, 0:D], bank(2 + n % 2)[:, 0:D], INV).then_inc(s_chi, 1)
                route_act(1, g)

            for g in range(G):
                front1(g)
            nc.scalar.preload_act_table(ACT.Silu)
            for g in range(G):
                tiles(1, g)

        @block.vector
        def _(dve):
            v = nc.vector
            chain = [0]

            def link(ins):
                chain[0] += 1
                ins.then_inc(s_dve, 1)
                dve.wait_ge(s_dve, chain[0])

            dve.wait_ge(s_const, 16)
            v.tensor_copy(ident16[:, :], ident)
            v.tensor_copy(identb[:, :], ident)
            v.tensor_copy(deltab[:, :], delta32)
            link(v.tensor_copy(ustrict16[:, :], cst[:, C_USTRICT:C_USTRICT + P]))
            dve.wait_ge(s_small, 16 * 19)
            dve.wait_ge(s_pads, 7)
            v.tensor_scalar(vsel[:, :], cst[:, C_VMASK:NCONST], vrep[:, 0:1], None, ALU.mult).then_inc(s_vsel, 1)
            dve.wait_ge(s_vt, 1)
            v.tensor_copy(vcols[:, :], bank(5)[:, 0:56]).then_inc(s_vcols, 1)
            link(v.tensor_scalar(selc[:, 0:1], ptc[:, :], 0.0, None, ALU.is_equal))
            link(v.tensor_scalar(selc[:, 1:2], ptc[:, :], 1.0, None, ALU.is_equal))
            link(v.tensor_tensor(selc[:, 3:4], selc[:, 0:1], selc[:, 1:2], ALU.add))
            link(v.tensor_scalar(selc[:, 2:3], selc[:, 3:4], -1.0, 1.0, ALU.mult, ALU.add))
            v.tensor_scalar(selb[:, 0, :], ptb[:, :], 0.0, None, ALU.is_equal)
            link(v.tensor_scalar(selb[:, 1, :], ptb[:, :], 1.0, None, ALU.is_equal))
            link(v.tensor_tensor(selb[:, 3, :], selb[:, 0, :], selb[:, 1, :], ALU.add))
            link(v.tensor_scalar(selb[:, 2, :], selb[:, 3, :], -1.0, 1.0, ALU.mult, ALU.add))
            link(v.tensor_scalar(cnt[:, :], selb[:, 0, :], cst[:, C_CNT:C_CNT + 1], None, ALU.mult))
            link(v.scalar_tensor_tensor(cnt[:, :], selb[:, 1, :], cst[:, C_CNT + 1:C_CNT + 2], cnt[:, :],
                                        ALU.mult, ALU.add))
            link(v.scalar_tensor_tensor(cnt[:, :], selb[:, 2, :], cst[:, C_CNT + 2:C_CNT + 3], cnt[:, :],
                                        ALU.mult, ALU.add))
            link(v.tensor_tensor(selb[:, 3, :], selb[:, 0, :], selb[:, 1, :], ALU.subtract))
            link(v.tensor_scalar(selb[:, 3, :], selb[:, 3, :], BIG, None, ALU.mult))
            link(v.tensor_scalar(selb[:, 2, :], selb[:, 2, :], BIG, None, ALU.mult))

            def masks(q):
                if q >= 2:
                    dve.wait_ge(s_arg, q - 1)
                for j in range(QB):
                    b = QB * q + j
                    v.tensor_scalar(mk[:, q % 2, 0, j * P:j * P + P], deltab[:, :], selb[:, 3, b:b + 1], 0.0,
                                    ALU.mult, ALU.max)
                    ins = v.tensor_scalar(mk[:, q % 2, 1, j * P:j * P + P], identb[:, :], selb[:, 2, b:b + 1],
                                          None, ALU.mult)
                ins.then_inc(s_mk, 1)

            dve.wait_ge(s_vcols, 1)
            v.tensor_scalar(vcols[:, 0:E0], vcols[:, 0:E0], WSCALE, None, ALU.mult).then_inc(s_vcols, 1)

            def split0(e):
                dve.wait_ge(s_rec0hi, e + 1)
                v.scalar_tensor_tensor(rec0[:, e, W1_LO:W1_LO + F], raw0[:, e % 2, 0:F], vcols[:, e:e + 1],
                                       rec0[:, e, W1_HI:W1_HI + F], ALU.mult, ALU.subtract)
                w2v = rec0[:, e, W2_AT:REC0].rearrange("p (c k n) -> p c k n", c=FC, k=2)
                v.scalar_tensor_tensor(w2v[:, :, 1, :], raw0[:, e % 2, F:2 * F].rearrange("p (c n) -> p c n", c=FC),
                                       WSCALE, w2v[:, :, 0, :], ALU.mult, ALU.subtract).then_inc(s_rec0, 1)

            masks(0)
            masks(1)
            link(v.tensor_scalar(r0h[:, 0, :], r0s[:, :], WSCALE, None, ALU.mult))
            v.scalar_tensor_tensor(r0h[:, 1, :], r0s[:, :], WSCALE, r0h[:, 0, :], ALU.mult, ALU.subtract)
            dve.wait_ge(s_vcols, 1)
            link(v.tensor_scalar(r1h[:, 0, :], vcols[:, 48:56], WSCALE, None, ALU.mult))
            v.scalar_tensor_tensor(r1h[:, 1, :], vcols[:, 48:56], WSCALE, r1h[:, 0, :], ALU.mult, ALU.subtract)
            bias = rec1[:, :, BIAS_AT:DB_AT].bitcast(F32)
            v.tensor_copy(bias[:, :, 0:FC], vcols[:, 16:32].rearrange("p (e c) -> p e c", c=FC))
            v.tensor_scalar(bias[:, :, FC:2 * FC], vcols[:, 32:48].rearrange("p (e c) -> p e c", c=FC),
                            WSCALE, None, ALU.mult)
            v.tensor_scalar(dbh[:, 0, :], dbr[:, :], WSCALE, None, ALU.mult).then_inc(s_db, 1)
            dve.wait_ge(s_db, 1)
            v.scalar_tensor_tensor(dbh[:, 1, :], dbr[:, :], WSCALE, dbh[:, 0, :], ALU.mult,
                                   ALU.subtract).then_inc(s_db, 1)
            dve.wait_ge(s_sc, 1)
            v.tensor_copy(ssb[:, :], bank(4)[0:B, 0:P]).then_inc(s_ssb, 1)
            mid = 64
            dve.wait_ge(s_ssb, 1)
            v.tensor_copy(mx[:, 0, mid:mid + P], ssb[:, :])
            link(v.tensor_copy(mx[:, 2, mid:mid + P], ssb[:, :]))
            at = 0
            for k in range(7):
                s = 1 << k
                v.tensor_tensor(mx[:, 1 - at, mid:mid + P], mx[:, at, mid:mid + P], mx[:, at, mid - s:mid - s + P],
                                ALU.max)
                link(v.tensor_tensor(mx[:, 3 - at, mid:mid + P], mx[:, 2 + at, mid:mid + P],
                                     mx[:, 2 + at, mid + s:mid + s + P], ALU.max))
                at = 1 - at
            dve.wait_ge(s_sTp, 1)
            v.tensor_copy(sT[:, :], bank(5)[:, 0:B]).then_inc(s_sT, 1)
            left, right, both = mx[:, at, :], mx[:, 2 + at, :], mx[:, 1 - at, mid:mid + P]
            link(v.tensor_scalar(mrow[:, :], left[:, mid:mid + P], selc[:, 0:1], None, ALU.mult))
            link(v.scalar_tensor_tensor(mrow[:, :], right[:, mid:mid + P], selc[:, 1:2], mrow[:, :],
                                        ALU.mult, ALU.add))
            link(v.tensor_tensor(both, left[:, mid - 1:mid - 1 + P], right[:, mid + 1:mid + 1 + P], ALU.max))
            v.scalar_tensor_tensor(mrow[:, :], both, selc[:, 2:3], mrow[:, :], ALU.mult, ALU.add).then_inc(s_max, 1)

            def copy_hT(q):
                dve.wait_ge(s_hTp, q + 1)
                v.tensor_copy(hT[:, :, q * QB * P:(q + 1) * QB * P],
                              bank16(4).rearrange("p (k t) -> p k t", k=2)).then_inc(s_hT, 1)

            def route(l, g):
                e, tm = NEXP[l], TM[l]
                gs = slice(g * NT, (g + 1) * NT)

                def over(a):
                    return a.unsqueeze(2).broadcast_to([P, NT, e])

                lge, dde, d2e, cde = lg[:, :, 0:e], dd[:, :, 0:e], d2[:, :, 0:e], cd[:, :, 0:e]
                iota = cst[:, C_IOTA:C_IOTA + e].unsqueeze(1).broadcast_to([P, NT, e])
                m2, e2x, mtop, code, zs, g1, g2, den = (sm[:, i, :] for i in range(8))
                if l == 0:
                    dve.wait_ge(s_lg[0], g + 1)
                    link(v.tensor_tensor(lge, bank(5)[:, 0:NT * e].rearrange("p (t e) -> p t e", e=e),
                                         over(sq[:, gs]), ALU.mult))
                else:
                    dve.wait_ge(s_lg[1], (g + 1) * NT)
                    link(v.tensor_copy(lge, bank(6)[:, 0:NT * e].rearrange("p (t e) -> p t e", e=e)))
                link(v.tensor_reduce(mtop, lge, AX.X, ALU.max))
                link(v.tensor_tensor(dde, lge, over(mtop), ALU.subtract))
                link(v.scalar_tensor_tensor(cde, dde, 0.0, iota, ALU.is_equal, ALU.mult))
                link(v.tensor_reduce(code, cde, AX.X, ALU.min))
                link(v.tensor_tensor(oh1[:, :, 0:e], iota, over(code), ALU.is_equal))
                link(v.scalar_tensor_tensor(d2e, oh1[:, :, 0:e], LOW, dde, ALU.mult, ALU.add))
                v.tensor_reduce(m2, d2e, AX.X, ALU.max).then_inc(s_diff[l], 1)
                dve.wait_ge(s_diff[l], g + 1)
                link(v.tensor_tensor(d2e, d2e, over(m2), ALU.subtract))
                link(v.scalar_tensor_tensor(cde, d2e, 0.0, iota, ALU.is_equal, ALU.mult))
                link(v.tensor_reduce(code, cde, AX.X, ALU.min))
                link(v.tensor_tensor(oh2[:, :, 0:e], iota, over(code), ALU.is_equal))
                v.tensor_tensor(oh16[:, :, 0:e], oh1[:, :, 0:e], oh2[:, :, 0:e], ALU.add).then_inc(s_oh[l], 1)
                dve.wait_ge(s_ex[l], g + 1)
                link(v.tensor_reduce(zs, ex[:, :, 0:e], AX.X, ALU.add))
                link(v.reciprocal(g1, zs))
                link(v.tensor_tensor(g2, e2x, g1, ALU.mult))
                link(v.tensor_tensor(den, g1, g2, ALU.add))
                link(v.tensor_scalar(den, den, 1e-9, None, ALU.add))
                link(v.reciprocal(den, den))
                v.scalar_tensor_tensor(gwt[:, l, 0, gs], g1, INV, den, ALU.mult, ALU.mult)
                link(v.scalar_tensor_tensor(gwt[:, l, 1, gs], g2, INV, den, ALU.mult, ALU.mult))
                dve.wait_ge(s_rank[l], g + 1)
                rb = rank_bank(l)
                link(v.tensor_copy(pre[:, 0, 16:16 + NT, 0:e],
                                   rb[:, 256:256 + NT * e].rearrange("p (t e) -> p t e", e=e)))
                at, s = 0, 1
                while s < NT:
                    link(v.tensor_tensor(pre[:, 1 - at, 16:16 + NT, 0:e], pre[:, at, 16:16 + NT, 0:e],
                                         pre[:, at, 16 - s:16 + NT - s, 0:e], ALU.add))
                    at, s = 1 - at, 2 * s
                link(v.tensor_scalar(nti[:, 0, 0:e], pre[:, at, 15 + NT, 0:e], SLOTS - 1.0, None, ALU.add))
                link(v.tensor_scalar(nti[:, 1, 0:e], nti[:, 0, 0:e], SLOTS.bit_length() - 1, None,
                                     ALU.logical_shift_right))
                link(v.tensor_copy(ntf[:, 0, 16:16 + e], nti[:, 1, 0:e]))
                a2, s = 0, 1
                while s < e:
                    link(v.tensor_tensor(ntf[:, 1 - a2, 16:16 + e], ntf[:, a2, 16:16 + e],
                                         ntf[:, a2, 16 - s:16 + e - s], ALU.add))
                    a2, s = 1 - a2, 2 * s
                upto = ntf[:, a2, :]
                tau = cst[0:1, C_TILE:C_TILE + tm].unsqueeze(2).broadcast_to([1, tm, e])
                ends = upto[0:1, 16:16 + e].unsqueeze(1).broadcast_to([1, tm, e])
                link(v.tensor_tensor(cmp_[:, 0:tm, 0:e], tau, ends, ALU.is_ge))
                link(v.tensor_reduce(tef[:, 0, 0:tm], cmp_[:, 0:tm, 0:e], AX.X, ALU.add))
                link(v.tensor_scalar(tef[:, 1, 0:tm], tef[:, 0, 0:tm], e - 1.0, None, ALU.min))
                link(v.tensor_copy(te[:, l, g, 0:tm], tef[:, 1, 0:tm]))
                link(v.tensor_scalar(cmp_base[:, 0:e], upto[:, 15:15 + e], float(SLOTS), None, ALU.mult))
                link(v.tensor_tensor(lge, rb[:, 0:NT * e].rearrange("p (t e) -> p t e", e=e),
                                     pre[:, at, 15:15 + NT, 0:e], ALU.add))
                link(v.tensor_tensor(lge, lge, cmp_base[:, 0:e].unsqueeze(1).broadcast_to([P, NT, e]), ALU.add))
                for k, oh in enumerate((oh1, oh2)):
                    link(v.tensor_tensor(cde, lge, oh[:, :, 0:e], ALU.mult))
                    link(v.tensor_reduce(sm[:, 8 + k, :], cde, AX.X, ALU.add))
                v.tensor_copy(idx[:, l, 0, gs], sm[:, 8, :])
                v.tensor_copy(idx[:, l, 1, gs], sm[:, 9, :]).then_inc(s_idx[l], 1)
                dve.wait_ge(s_idx[l], g + 1)

            for g in range(G):
                q0, q1 = g * NQ // G, (g + 1) * NQ // G
                for q in range(q0, q1):
                    dve.wait_ge(s_pool, q + 1)
                    o = ps[:, 2 * (q % 2):2 * (q % 2) + 2, :].rearrange("p a (b c) -> p a b c", b=2)
                    bs = slice(QB * q, QB * q + QB)
                    link(v.tensor_tensor(rc[:, bs].rearrange("p (a b) -> p a b", a=2), o[:, :, :, D],
                                         cnt[:, bs].rearrange("p (a b) -> p a b", a=2), ALU.mult))
                    link(v.reciprocal(rc[:, bs], rc[:, bs]))
                    v.tensor_tensor(pooled[:, bs, :].rearrange("p (a b) d -> p a b d", a=2), o[:, :, :, 0:D],
                                    rc[:, bs].rearrange("p (a b) -> p a b", a=2).unsqueeze(3).broadcast_to([P, 2, 2, D]),
                                    ALU.mult).then_inc(s_pooled, 1)
                    if q + 2 < NQ:
                        masks(q + 2)
                    split0(2 * q)
                    split0(2 * q + 1)
                gs = slice(g * NT, (g + 1) * NT)
                dve.wait_ge(s_ssq, q1)
                v.tensor_scalar(rr[:, gs], ssq[:, gs], 1.0 / D, 1.1920929e-07, ALU.mult, ALU.add).then_inc(s_ms, 1)
                dve.wait_ge(s_sqrt, g + 1)
                link(v.reciprocal(rr[:, gs], sq[:, gs]))
                for q in range(q0, q1):
                    bs = slice(QB * q, QB * q + QB)
                    v.tensor_tensor(pooled[:, bs, :], pooled[:, bs, :],
                                    rr[:, bs].unsqueeze(2).broadcast_to([P, QB, D]), ALU.mult).then_inc(s_h0, 1)
                    dve.wait_ge(s_hhi, q + 1)
                    v.tensor_tensor(hl[:, bs, D:2 * D], pooled[:, bs, :], hl[:, bs, 0:D],
                                    ALU.subtract).then_inc(s_hlo, 1)
                    if q > q0:
                        copy_hT(q - 1)
                copy_hT(q1 - 1)
                route(0, g)

            def shared_split(n):
                j, k = n % 2, n // 2
                dve.wait_ge(s_sS, n + 1)
                if k >= 1:
                    dve.wait_ge(s_sD, k)
                v.tensor_copy(hh[:, j, :], hf[:, j, :]).then_inc(s_sHi, 1)
                dve.wait_ge(s_sHi, n + 1)
                v.tensor_tensor(hlo[:, j, :], hf[:, j, :], hh[:, j, :], ALU.subtract).then_inc(s_sLo, 1)

            def shared_add(k):
                dve.wait_ge(s_sD, k + 1)
                xq = xs[:, QB * k:QB * k + QB, 0:D]
                v.scalar_tensor_tensor(xq, bank(6 + k % 2).rearrange("p (t d) -> p t d", d=D), INV, xq,
                                       ALU.mult, ALU.add).then_inc(s_sY, 1)

            def split_w(e):
                dve.wait_ge(s_rec1hi, e + 1)
                r = raw1[:, e % 2, :]
                gu = rec1[:, e, 0:4 * F].rearrange("p (m k f) -> p m k f", m=2, k=2)
                v.scalar_tensor_tensor(gu[:, :, 1, :], r[:, 0:2 * F].rearrange("p (m f) -> p m f", m=2), WSCALE,
                                       gu[:, :, 0, :], ALU.mult, ALU.subtract)
                dn = rec1[:, e, DN_AT:BIAS_AT].rearrange("p (c k n) -> p c k n", c=FC, k=2)
                v.scalar_tensor_tensor(dn[:, :, 1, :], r[:, 2 * F:3 * F].rearrange("p (c n) -> p c n", c=FC), WSCALE,
                                       dn[:, :, 0, :], ALU.mult, ALU.subtract)
                v.scalar_tensor_tensor(wc[:, 4 * e:4 * e + 4, D:2 * D], r[:, 3 * F:].rearrange("p (b n) -> p b n", b=4),
                                       WSCALE, wc[:, 4 * e:4 * e + 4, 0:D], ALU.mult, ALU.subtract).then_inc(s_rec1, 1)

            for k in range(NQ):
                shared_split(2 * k)
                shared_split(2 * k + 1)
                if k >= 1:
                    shared_add(k - 1)
                split_w(k)
            shared_add(NQ - 1)

            def tiles(l, g):
                s = L[l]
                base, tm = g * TM[l], TM[l]
                W = FC * SLOTS

                def split(n, slot, b):
                    dve.wait_ge(s["silu"], n + 1 + CREDIT)
                    h32 = hf[:, b, 0:W]
                    if l == 1:
                        for c in range(FC):
                            f = slice(c * SLOTS, (c + 1) * SLOTS)
                            ub_ = wr[:, slot, BIAS_AT + 2 * (FC + c):BIAS_AT + 2 * (FC + c) + 2].bitcast(F32)
                            ins = v.scalar_tensor_tensor(hf[:, b, f], bank(3 + 2 * b)[:, f], ub_,
                                                         hf[:, b, (2 + c) * SLOTS:(3 + c) * SLOTS], ALU.add, ALU.mult)
                        ins.then_inc(s["h"], 1)
                        dve.wait_ge(s["h"], n + 1 + CREDIT)
                    dve.wait_ge(s["D"], n + 3)
                    if l == 0:
                        v.tensor_copy(hh[:, b, 0:W], h32).then_inc(s["hi"], 1)
                    else:
                        v.tensor_scalar(hh[:, b, 0:W], h32, INV, None, ALU.mult).then_inc(s["hi"], 1)
                    dve.wait_ge(s["hi"], n + 1 + CREDIT)
                    if l == 0:
                        v.tensor_tensor(hlo[:, b, 0:W], h32, hh[:, b, 0:W], ALU.subtract).then_inc(s["lo"], 1)
                    else:
                        v.scalar_tensor_tensor(hlo[:, b, 0:W], h32, INV, hh[:, b, 0:W], ALU.mult,
                                               ALU.subtract).then_inc(s["lo"], 1)

                def y_copy(n, k, turn):
                    dve.wait_ge(s["D"], n + 1 + CREDIT)
                    if k % 2 == 0:
                        dve.wait_ge(s["st"][k // 2 % 2], 16 * (k // 4 + turn + 1))
                    v.tensor_copy(ys[:, k % YRING, :, :].rearrange("p h d -> p (h d)"),
                                  bank(6 + k % 2)[:, 0:HALVES * D]).then_inc(s["y"], 1)

                def step(i0, turn):
                    loop = type(turn) is not int
                    off = WRING * turn if loop else 0
                    if loop or i0 < tm:
                        n = base + i0
                        split(n + off, n % WRING, n % 2)
                    if l == 0 and (loop or i0 >= 1):
                        n = base + i0 - 1
                        y_copy(n + off, n, turn)
                step(0, 0)
                loops = (tm - 2) // WRING
                with dve.Fori(0, loops) as turn:
                    for j in range(WRING):
                        step(1 + j, turn)
                for i in range(1 + loops * WRING, tm + 1):
                    step(i, 0)

            for g in range(G):
                tiles(0, g)

            def combine(l, b):
                n = l * B + b
                dve.wait_ge(s_gr[n % RRING], 32 * (n // RRING + 1))
                xb = xs[:, b, 0:D]
                link(v.scalar_tensor_tensor(xb, gr[:, n % RRING, 0, :], gwt[:, l, 0, b:b + 1], xb, ALU.mult, ALU.add))
                v.scalar_tensor_tensor(xb, gr[:, n % RRING, 1, :], gwt[:, l, 1, b:b + 1], xb,
                                       ALU.mult, ALU.add).then_inc(s_x1, 1)

            def front1(g):
                for t in range(NT + 2):
                    if t < NT:
                        b = n = g * NT + t
                        combine(0, b)
                        dve.wait_ge(s_xhi, n + 1)
                        v.tensor_tensor(xs16[:, n % 2, D:2 * D], xs[:, b, 0:D], xs16[:, n % 2, 0:D],
                                        ALU.subtract).then_inc(s_xlo, 1)
                    if 0 <= t - 1 < NT:
                        b = n = g * NT + t - 1
                        dve.wait_ge(s_chi, n + 1)
                        v.scalar_tensor_tensor(hl[:, b, D:2 * D], bank(2 + n % 2)[:, 0:D], INV, hl[:, b, 0:D],
                                               ALU.mult, ALU.subtract).then_inc(s_clo, 1)
                    if 0 <= t - 2 < NT:
                        b = n = g * NT + t - 2
                        dve.wait_ge(s_t3, n + 1)
                        if n >= 2:
                            dve.wait_ge(s_lg[1], n - 1)
                        v.tensor_copy(ctt[:, n % 2, :], bank16(4 + n % 2)[:, 0:2 * P]).then_inc(s_ctt, 1)
                route(1, g)

            for g in range(G):
                front1(g)
            for g in range(G):
                tiles(1, g)
            for b in range(B):
                combine(1, b)


_INS = ['x', 'itok_B_0_2', 'itok_B_0_30', 'L0_cond_W1', 'L0_cond_b1', 'L0_cond_v', 'L0_ffn_router_w', 'L0_ffn_rms_w',
        'L0_ffn_w1', 'L0_ffn_w2', 'L0_ffn_rms_w_s', 'L0_ffn_w1_s', 'L0_ffn_w2_s', 'L1_cond_W', 'L1_cond_b',
        'L1_ffn_router_w', 'L1_ffn_gate_w', 'L1_ffn_gate_b', 'L1_ffn_up_w', 'L1_ffn_up_b', 'L1_ffn_down_w',
        'L1_ffn_down_b']


def kernel(**inputs):
    import concourse.bacc as bacc
    from concourse.bass_utils import run_bass_kernel_spmd

    nc = bacc.Bacc("TRN2", target_bir_lowering=False, num_devices=1)
    arrays, args = {}, []
    for name in _INS + ["constants"]:
        a = np.ascontiguousarray(constants() if name == "constants" else inputs[name])
        arrays[f"in_{name}"] = a
        args.append(nc.dram_tensor(f"in_{name}", a.shape, mybir.dt.from_np(a.dtype), kind="ExternalInput").ap())
    args.append(nc.dram_tensor("out_x", (B, P, D), F32, kind="ExternalOutput").ap())
    build(nc, *args)
    r = run_bass_kernel_spmd(nc, [arrays], core_ids=[0])
    return r.results[0]["out_x"]
```

```python
from contextlib import ExitStack

import numpy as np

import concourse.bass as bass
from concourse import mybir

ALU = mybir.AluOpType
ACT = mybir.ActivationFunctionType
AX = mybir.AxisListType
F32 = mybir.dt.float32
F16 = mybir.dt.float16
BF16 = mybir.dt.bfloat16
I32 = mybir.dt.int32

P = 128
D = 128
B = 32
A = 32
F = 256
FC = F // P
ER, ES = 14, 2
E0 = ER + ES
E1 = 8
G = 2
NT = B // G
SLOTS = 256
HALVES = SLOTS // P
NEXP = (ER, E1)
TM = tuple(((NT * P * 2 + e * (SLOTS - 1)) // SLOTS + 1) // 2 * 2 for e in NEXP)
QB = 4
NQ = B // QB
WSCALE = 256.0
INV = 1.0 / WSCALE
BIG = 2.0 ** 100
LOW = -1e30
ICODE = 64.0

W1_HI, W1_LO = 0, F
W2_AT = 2 * F
REC0 = W2_AT + FC * 2 * D
G_HI, G_LO, U_HI, U_LO = 0, F, 2 * F, 3 * F
DN_AT = 4 * F
BIAS_AT = DN_AT + FC * 2 * D
DB_AT = BIAS_AT + 8
REC1 = DB_AT + D
WRING = 4
YRING = 4
RAWS = 6
RRING = 4

C_IDENT, C_USTRICT, C_DELTA = 0, 128, 256
C_CNT, C_IOTA, C_TILE, C_VMASK = 384, 387, 403, 435
NCONST = C_VMASK + 2 * 4 * B

CREDIT = 4


def constants():
    c = np.zeros((P, NCONST), np.float32)
    p = np.arange(P)
    c[:, C_IDENT:C_IDENT + P] = np.eye(P)
    c[:, C_USTRICT:C_USTRICT + P] = p[:, None] < p[None, :]
    c[:, C_DELTA:C_DELTA + P] = p[:, None] - p[None, :]
    c[:, C_CNT] = p + 1
    c[:, C_CNT + 1] = P - p
    c[:, C_CNT + 2] = P - 1
    c[:, C_IOTA:C_IOTA + 16] = np.arange(16) - ICODE
    c[:, C_TILE:C_TILE + 32] = np.arange(32)
    vm = c[:, C_VMASK:].reshape(P, 2, 4, B)
    for h in range(2):
        for bb in range(4):
            for g in range(4):
                vm[32 * g:32 * g + 32, h, bb, 16 * h + 4 * g + bb] = 1
    return c


def build(nc, x, ptype, cat, cw1, cb1, cv, rtr0, rms, w1, w2, rms_s, w1s, w2s, cW, cb,
          rtr1, gw, gb, uw, ub, dw, db, const, out):
    rows_d = [nc.dram_tensor(f"rows_{g}", [max(TM) * SLOTS, 2 * D], F16).ap() for g in range(G)]
    y_d = [nc.dram_tensor(f"expert_out_{g}", [max(TM) * SLOTS, D], F32).ap() for g in range(G)]

    with ExitStack() as ctx:
        def sb(name, shape, dt=F32):
            return ctx.enter_context(nc.sbuf_tensor(name, shape, dt))

        def sem(name):
            return ctx.enter_context(nc.semaphore(name))

        cst = sb("constants", [P, NCONST])
        ident, delta32 = cst[:, C_IDENT:C_IDENT + P], cst[:, C_DELTA:C_DELTA + P]
        ident16 = sb("ident16", [P, P], F16)
        ustrict16 = sb("ustrict16", [P, P], F16)
        ones16 = sb("ones16", [P, P], F16)
        identb = sb("identb", [P, P], BF16)
        deltab = sb("deltab", [P, P], BF16)
        NC = cb.shape[0]
        catb, cbt = sb("cat_all", [NC, B], I32), sb("cond_b", [NC, D])
        is_cat = sb("is_category", [NC, B])
        xs = sb("x_rows", [P, B, D + 2])
        xT = sb("xT", [P, B * P])
        pooled = xT[:, :].rearrange("p (b d) -> p b d", b=B)
        hl = sb("rows_hl", [P, B, 2 * D], F16)
        hT = sb("hT", [P, 2, B * P], F16)
        rec0 = sb("records0", [P, E0, REC0], F16)
        rec1 = sb("records1", [P, E1, REC1], F16)
        wr = sb("record_ring", [P, WRING, REC1], F16)
        STG = 3 * F + 4 * D
        raw1 = wr[:, :, :].rearrange("p a c -> p (a c)")[:, 0:2 * 2 * STG].bitcast(F32).rearrange(
            "p (s c) -> p s c", s=2)
        wc = sb("cond_w", [P, B, 2 * D], F16)
        rowr = sb("row_ring", [P, RRING, HALVES, 2 * D], F16)
        xt = sb("xt", [P, 2, 2, SLOTS], F16)
        hf = sb("hidden32", [P, 2, 4 * SLOTS])
        hh = sb("hidden_hi", [P, 2, 4 * SLOTS], F16)
        hlo = sb("hidden_lo", [P, 2, 4 * SLOTS], F16)
        PT = hf[:, :, 0:QB * P]
        mk = hf[:, :, QB * P:2 * QB * P].bitcast(BF16).rearrange("p s (k c) -> p s k c", k=2)
        ys = sb("y_rows", [P, YRING, HALVES, D])
        raw0 = wr[:, :, :].rearrange("p a c -> p (a c)")[:, 0:RAWS * 4 * F].bitcast(F32).rearrange(
            "p (s c) -> p s c", s=RAWS)
        attn = hh[:, :, :].rearrange("p a c -> p (a c)").bitcast(F32).rearrange(
            "p (a c) -> p a c", a=2)
        hh4, hlo4 = (v[:, :, :].rearrange("p a (k c) -> p (a k) c", k=2) for v in (hh, hlo))
        got0 = xT[:, :].rearrange("p (b k d) -> p b k d", k=2, d=D)
        got1 = rec0[:, :, :].rearrange("p e c -> p (e c)").bitcast(F32).rearrange("p (b k d) -> p b k d", k=2, d=D)

        def gathered(l, b):
            return got0[:, b] if l == 0 and b < NT else got1[:, b]
        mx = rowr[0:B, :, :, :].rearrange("p s h c -> p s (h c)").bitcast(F32)
        mrow = sb("row_max", [B, P])
        sT = sb("scores_t", [P, B])
        zeros = wc[:, :, :].rearrange("p b c -> p (b c)")[:, 0:max(TM) * SLOTS * 2 * D // P // 8]
        vrep = sb("v_rep", [P, 1])
        brep = sb("b1_rep", [P, 1])
        xt32 = xt[:, :, :, :].rearrange("p a k s -> p (a k s)").bitcast(F32)
        vsel = xt32[:, 0:2 * 4 * B]
        cw1s = sb("cond_w1", [P, A])
        ptc, ptb = sb("ptype_col", [B, 1], I32), sb("ptype_all", [P, B], I32)
        catr = sb("cat_row", [1, B], I32)
        selc = sb("sel_col", [B, 4])
        selb = sb("sel_all", [P, 4, B])
        cnt = sb("count", [P, B])
        rc = sb("pool_recip", [P, B])
        ssq = sb("sum_sq", [P, B])
        sq = sb("rms", [P, B])
        rr = sb("rms_recip", [P, B])
        squares_out = hlo[:, 1, :].bitcast(F32)
        vrows, ssb = xt32[0:56, 2 * P:3 * P], xt32[0:B, 3 * P:4 * P]
        vcols = sb("vector_cols", [P, 56])
        r0s, r0h = sb("router0", [P, ER]), sb("router0_hl", [P, 2, ER], F16)
        r1h = sb("router1_hl", [P, 2, E1], F16)
        dbr, dbh = sb("down_b", [E1, D]), sb("down_b_hl", [E1, 2, D], F16)
        lg, dd, d2 = sb("logits", [P, NT, 16]), sb("diff", [P, NT, 16]), sb("diff2", [P, NT, 16])
        ex, cd = sb("expd", [P, NT, 16]), sb("code", [P, NT, 16])
        oh1, oh2 = sb("onehot1", [P, NT, 16]), sb("onehot2", [P, NT, 16])
        oh16 = sb("onehot", [P, NT, 16], F16)
        sm = sb("small", [P, 12, NT])
        pre = sb("tile_prefix", [P, 2, 16 + NT, 16])
        nti, ntf = sb("tiles_int", [P, 2, 16], I32), sb("tiles", [P, 2, 32])
        cmp_ = sb("tile_cmp", [1, 32, 16])
        cmp_base = sb("first_slot", [P, 16])
        tef = sb("tile_expert_f", [1, 2, 32])
        te = sb("tile_expert", [1, 2, G, 32], I32)
        gwt = sb("gate_weights", [P, 2, 2, B])
        idx = sb("slot_index", [P, 2, 2, B], I32)
        xs16, xtt = (hh[:, 0, k * 4 * D:(k + 1) * 4 * D].rearrange("p (s c) -> p s c", s=2) for k in range(2))
        ctt = hh[:, 1, 0:4 * D].rearrange("p (s c) -> p s c", s=2)

        ps = ctx.enter_context(nc.psum_tensor("ps", [P, 8, 512], F32))

        def bank(n):
            return ps[:, n, :]

        def rank_bank(l):
            return bank(7 if l else 4)

        def bank16(n):
            return ps[:, n, :].bitcast(F16)

        s_const = sem("s_const"); s_small = sem("s_small"); s_late = sem("s_late"); s_av = sem("s_av"); s_x = [sem(f"s_xin{q}") for q in range(NQ)]
        s_zero = sem("s_zero"); s_zfill = sem("s_zfill"); s_pads = sem("s_pads"); s_tab = sem("s_tab")
        s_dve = sem("s_dve"); s_ms = sem("s_ms"); s_act = sem("s_act")
        s_raw0 = [sem(f"s_raw0_{i}") for i in range(RAWS)]; s_rec0 = sem("s_rec0"); s_rec0hi = sem("s_rec0hi")
        s_raw1 = [sem(f"s_raw1_{i}") for i in range(2)]; s_rec1hi = sem("s_rec1hi"); s_rec1 = sem("s_rec1")
        s_vt = sem("s_vt"); s_vcols = sem("s_vcols"); s_db = sem("s_db"); s_dbrow = sem("s_dbrow")
        s_xTp = sem("s_xTp"); s_xT = sem("s_xT"); s_pa = sem("s_pa"); s_tanh = sem("s_tanh")
        s_vsel = sem("s_vsel"); s_sc = sem("s_sc"); s_ssb = sem("s_ssb"); s_sTp = sem("s_sTp"); s_sT = sem("s_sT")
        s_max = sem("s_max"); s_mk = sem("s_mk"); s_arg = sem("s_arg"); s_pt = sem("s_pt")
        s_pool = sem("s_pool"); s_pooled = sem("s_pooled"); s_ssq = sem("s_ssq"); s_sqrt = sem("s_sqrt")
        s_h0 = sem("s_h0"); s_hhi = sem("s_hhi"); s_hlo = sem("s_hlo"); s_hTp = sem("s_hTp"); s_hT = sem("s_hT")
        s_lg = [sem("s_lg0"), sem("s_lg1")]; s_diff = [sem("s_diff0"), sem("s_diff1")]
        s_ex = [sem("s_ex0"), sem("s_ex1")]; s_oh = [sem("s_oh0"), sem("s_oh1")]
        s_rank = [sem("s_rank0"), sem("s_rank1")]; s_idx = [sem("s_idx0"), sem("s_idx1")]
        s_scat = [[sem(f"s_scat{l}_{g}") for g in range(G)] for l in range(2)]
        s_sU = sem("s_sU"); s_sS = sem("s_sS"); s_sHi = sem("s_sHi"); s_sLo = sem("s_sLo")
        s_sD = sem("s_sD"); s_sY = sem("s_sY")
        L = [dict(rows=[sem(f"l{l}_rows{i}") for i in range(RRING // 2)],
                  w=[sem(f"l{l}_w{i}") for i in range(WRING)],
                  st=[sem(f"l{l}_store{i}") for i in range(YRING // 2)],
                  **{k: sem(f"l{l}_{k}") for k in ("T", "xt", "U", "silu", "h", "hi", "lo", "D", "y")})
             for l in range(2)]
        s_gr = [sem(f"s_gather{k}") for k in range(B // 2)]
        s_x1 = sem("s_x1"); s_xhi = sem("s_xhi"); s_xlo = sem("s_xlo"); s_t2 = sem("s_t2"); s_xtt = sem("s_xtt")
        s_c = sem("s_c"); s_chi = sem("s_chi"); s_clo = sem("s_clo"); s_t3 = sem("s_t3"); s_ctt = sem("s_ctt")
        s_iscat = sem("s_iscat"); s_out = sem("s_out"); s_credit = sem("s_credit")

        block = ctx.enter_context(nc.Block())

        @block.sync
        def _(sp):
            sp.dma_start(cst[:, :], const).then_inc(s_const, 16)
            for q in range(2):
                sp.dma_start(xs[:, QB * q:QB * q + QB, 0:D],
                             x[QB * q:QB * q + QB].rearrange("b p d -> p b d")).then_inc(s_x[q], 16)
            sp.dma_start(cw1s[:, :], cw1).then_inc(s_small, 16)
            sp.dma_start(ptc[:, :], ptype.rearrange("(a o) -> a o", o=1)).then_inc(s_small, 16)
            sp.dma_start(ptb[:, :], ptype.rearrange("(o a) -> o a", o=1).broadcast_to([P, B])).then_inc(s_small, 16)
            for q in range(2, NQ):
                sp.dma_start(xs[:, QB * q:QB * q + QB, 0:D],
                             x[QB * q:QB * q + QB].rearrange("b p d -> p b d")).then_inc(s_x[q], 16)
            for e in range(E0):
                if e >= RAWS:
                    sp.wait_ge(s_rec0, e - RAWS + 1)
                a, b_ = (w1[e], w2[e]) if e < ER else (w1s[e - ER], w2s[e - ER])
                sp.dma_start(raw0[:, e % RAWS, 0:F], a).then_inc(s_raw0[e % RAWS], 16)
                sp.dma_start(raw0[:, e % RAWS, F:2 * F].rearrange("p (c n) -> p c n", c=FC),
                             b_.rearrange("(c p) n -> p c n", p=P)).then_inc(s_raw0[e % RAWS], 16)
                if e == RAWS - 1:
                    sp.wait_ge(s_zero, 1)
                    for g in range(G):
                        n = zeros.shape[1]
                        sp.dma_start(rows_d[g].rearrange("(p r) c -> p (r c)", p=P).rearrange("p (k n) -> p k n", n=n),
                                     zeros[:, :].unsqueeze(1).broadcast_to([P, 8, n])).then_inc(s_zfill, 16)
            sp.wait_ge(s_db, 2)
            sp.dma_start(rec1[0:1, :, DB_AT:DB_AT + D], dbh[:, 0, :]).then_inc(s_dbrow, 16)
            sp.dma_start(rec1[1:2, :, DB_AT:DB_AT + D], dbh[:, 1, :]).then_inc(s_dbrow, 16)
            sp.wait_ge(s_rec0, E0)
            for e in range(E1):
                if e >= 2:
                    sp.wait_ge(s_rec1, e - 1)
                for k, w in enumerate((gw, uw)):
                    sp.dma_start(raw1[:, e % 2, k * F:k * F + F], w[e]).then_inc(s_raw1[e % 2], 16)
                sp.dma_start(raw1[:, e % 2, 2 * F:3 * F].rearrange("p (c n) -> p c n", c=FC),
                             dw[e].rearrange("(c p) n -> p c n", p=P)).then_inc(s_raw1[e % 2], 16)
                if e == 0:
                    sp.wait_ge(s_late, 16 * 10)
                for j in range(4):
                    b = 4 * e + j
                    c = sp.value_load(catr[0:1, b:b + 1], min_val=0, max_val=cW.shape[0] - 1)
                    sp.dma_start(raw1[:, e % 2, 3 * F + j * D:3 * F + j * D + D],
                                 cW[bass.ds(c, 1), :, :].rearrange("a p d -> (a p) d")).then_inc(s_raw1[e % 2], 16)

            def records(l, g):
                rec, nrec, s = (rec0, REC0, L[0]) if l == 0 else (rec1, REC1, L[1])
                base, tm = g * TM[l], TM[l]

                def load_record(i, j):
                    off = WRING * i if type(i) is not int else 0
                    slot = (base + j) % WRING
                    e = sp.value_load(te[0:1, l, g, bass.ds(j + off, 1)], min_val=0, max_val=NEXP[l] - 1)
                    sp.wait_ge(s["D"], base + j + 1 + off)
                    sp.dma_start(wr[:, slot, 0:nrec].bitcast(I32),
                                 rec[:, bass.ds(e, 1), :].rearrange("p a c -> p (a c)").bitcast(I32)).then_inc(
                                     s["w"][slot], 16)
                sp.wait_ge(s_idx[l], g + 1)
                loops = tm // WRING
                with sp.Fori(0, loops) as turn:
                    for j in range(WRING):
                        load_record(turn, j)
                for j in range(WRING * loops, tm):
                    load_record(0, j)

            sp.wait_ge(s_rec1, E1)
            sp.wait_ge(s_dbrow, 32)
            sp.wait_ge(s_credit, 1)
            for g in range(G):
                records(0, g)
            for g in range(G):
                records(1, g)
            for q in range(NQ):
                sp.wait_ge(s_x1, B + QB * (q + 1))
                sp.dma_start(out[QB * q:QB * q + QB].rearrange("b p d -> p b d"),
                             xs[:, QB * q:QB * q + QB, 0:D]).then_inc(s_out, 16)
            sp.wait_ge(s_out, 16 * NQ)

        @block.gpsimd
        def _(pool):
            nc.gpsimd.memset(zeros[:, :], 0.0).then_inc(s_zero, 1)
            nc.gpsimd.memset(mx[:, :, :], LOW).then_inc(s_pads, 1)
            nc.gpsimd.memset(xs[:, :, D:D + 2], 1.0).then_inc(s_pads, 1)
            nc.gpsimd.memset(pre[:, :, :, :], 0.0).then_inc(s_pads, 1)
            nc.gpsimd.memset(ntf[:, :, :], 0.0).then_inc(s_pads, 1)
            nc.gpsimd.memset(rec1[:, :, DB_AT:DB_AT + D], 0.0).then_inc(s_pads, 1)
            nc.gpsimd.memset(ones16[:, :], 1.0).then_inc(s_pads, 1)
            nc.gpsimd.dma_start(catr[:, :], cat.rearrange("(o a) -> o a", o=1)).then_inc(s_late, 16)
            nc.gpsimd.dma_start(vrows[0:14, :], rms).then_inc(s_late, 16)
            nc.gpsimd.dma_start(vrows[14:16, :], rms_s).then_inc(s_late, 16)
            nc.gpsimd.dma_start(vrows[16:32, :], gb.rearrange("e (c p) -> (e c) p", p=P)).then_inc(s_late, 16)
            nc.gpsimd.dma_start(vrows[32:48, :], ub.rearrange("e (c p) -> (e c) p", p=P)).then_inc(s_late, 16)
            nc.gpsimd.dma_start(vrows[48:56, :], rtr1).then_inc(s_late, 16)
            nc.gpsimd.dma_start(r0s[:, :], rtr0).then_inc(s_late, 16)
            nc.gpsimd.dma_start(dbr[:, :], db).then_inc(s_late, 16)
            nc.gpsimd.dma_start(catb[:, :], cat.rearrange("(o a) -> o a", o=1).broadcast_to([NC, B])).then_inc(s_late, 16)
            nc.gpsimd.dma_start(cbt[:, :], cb).then_inc(s_late, 16)

            def scatter(l, g):
                if l == 0:
                    pool.wait_ge(s_zfill, 16 * G)
                    pool.wait_ge(s_hlo, (g + 1) * NT // QB)
                else:
                    pool.wait_ge(s_clo, (g + 1) * NT)
                    for k in range(RRING // 2):
                        pool.wait_ge(L[0]["rows"][k], 16 * len(
                            [t for t in range(0, (g + 1) * TM[0], 2) if t // 2 % (RRING // 2) == k]))
                pool.wait_ge(s_idx[l], g + 1)
                for t in range(NT):
                    b = g * NT + t
                    for k in range(2):
                        nc.gpsimd.indirect_dma_start(
                            rows_d[g], bass.IndirectOffsetOnAxis(ap=idx[:, l, k, b:b + 1], axis=0),
                            hl[:, b, :], None).then_inc(s_scat[l][g], 16)

            def gather(l, g):
                if l == 1 and g == 0:
                    pool.wait_ge(s_x1, B)
                for k in range(2):
                    stored = len([t for t in range(0, (g + 1) * TM[l], 2) if t // 2 % 2 == k])
                    pool.wait_ge(L[l]["st"][k], 16 * (stored + 1))
                for t in range(NT):
                    b = g * NT + t
                    for k in range(2):
                        nc.gpsimd.indirect_dma_start(
                            gathered(l, b)[:, k, :], None, y_d[g],
                            bass.IndirectOffsetOnAxis(ap=idx[:, l, k, b:b + 1], axis=0)).then_inc(s_gr[b // 2], 16)

            for s in L:
                for k in ("T", "xt", "U", "silu", "h", "hi", "lo", "D", "y"):
                    pool.sem_inc(s[k], CREDIT)
                for k in range(2):
                    pool.sem_inc(s["st"][k], 16)
            pool.sem_inc(s_credit, 1)
            for g in range(G):
                scatter(0, g)
            for g in range(G):
                gather(0, g)
                if g > 0:
                    scatter(1, g - 1)
            scatter(1, G - 1)
            for g in range(G):
                gather(1, g)

        @block.tensor
        def _(pe):
            pe.wait_ge(s_const, 16)
            for q in range(NQ + 1):
                if q < NQ:
                    pe.wait_ge(s_x[q], 16)
                    if q >= 2:
                        pe.wait_ge(s_xT, q - 1)
                    for j in range(QB):
                        mm = pe.transpose(bank(q % 2)[:, j * P:j * P + P], xs[:, QB * q + j, 0:D], ident)
                    mm.then_inc(s_xTp, 1)
                if q >= 1:
                    k = q - 1
                    if q == 1:
                        pe.wait_ge(s_small, 16 * 3)
                    pe.wait_ge(s_xT, k + 1)
                    h, g = k // 4, k % 4
                    mm = pe.matmul(ps[32 * g:32 * g + 32, 2 + h, :], cw1s[:, :],
                                   xT[:, k * QB * P:(k + 1) * QB * P], start=True, stop=True)
                    if g == 3:
                        mm.then_inc(s_pa, 1)
            pe.wait_ge(s_vsel, 1)
            for h in range(2):
                pe.wait_ge(s_tanh, h + 1)
                for bb in range(4):
                    mm = pe.matmul(bank(4)[0:B, 0:P], vsel[:, (4 * h + bb) * B:(4 * h + bb + 1) * B],
                                   attn[:, h, bb * P:bb * P + P], start=(h + bb == 0), stop=(h + bb == 4))
            mm.then_inc(s_sc, 1)
            pe.wait_ge(s_ssb, 1)
            pe.transpose(bank(5)[:, 0:B], ssb[:, :], ident[0:B, 0:B]).then_inc(s_sTp, 1)
            pe.wait_ge(s_late, 16 * 10)
            pe.transpose(bank(4)[:, 0:56], vrows[:, :], ident[0:56, 0:56]).then_inc(s_vt, 1)
            pe.wait_ge(s_max, 1)

            def exponent(q):
                pe.wait_ge(s_mk, q + 1)
                if q >= 2:
                    pe.wait_ge(s_pt, q - 1)
                o = bank(6 + q % 2)
                for j in range(QB):
                    b = QB * q + j
                    pe.matmul(o[:, j * P:j * P + P], ident[0:B, b:b + 1].broadcast_to([B, P]), mrow[:, :],
                              start=(j == 0), stop=False, skip_group_check=True)
                pe.matmul(o, identb[:, :], mk[:, q % 2, 0, :], start=False, stop=False, skip_group_check=True)
                mm = pe.matmul(o, identb[:, :], mk[:, q % 2, 1, :], start=False, stop=True, skip_group_check=True)
                mm.then_inc(s_arg, 1)

            def pool_mm(q):
                pe.wait_ge(s_pt, q + 1)
                if q >= 2:
                    pe.wait_ge(s_pooled, q - 1)
                for j in range(QB):
                    mm = pe.matmul(ps[:, 2 * (q % 2) + j // 2, 256 * (j % 2):256 * (j % 2) + D + 1],
                                   PT[:, q % 2, j * P:j * P + P], xs[:, QB * q + j, 0:D + 1], start=True, stop=True)
                mm.then_inc(s_pool, 1)

            def rank_mm(l, g):
                pe.wait_ge(s_oh[l], g + 1)
                n, e = NT * NEXP[l], NEXP[l]
                o = oh16[:, :, 0:e]
                pe.matmul(rank_bank(l)[:, 0:n], ustrict16[:, :], o, start=True, stop=True)
                pe.matmul(rank_bank(l)[:, 256:256 + n], ones16[:, :], o, start=True, stop=True).then_inc(s_rank[l], 1)

            for g in range(G):
                q0, q1 = g * NQ // G, (g + 1) * NQ // G
                exponent(q0)
                for q in range(q0, q1):
                    if q + 1 < q1:
                        exponent(q + 1)
                    pool_mm(q)
                for q in range(q0, q1):
                    pe.wait_ge(s_hlo, q + 1)
                    if q >= 1:
                        pe.wait_ge(s_hT, q)
                    if g >= 1 and q == q0:
                        pe.wait_ge(s_idx[0], g)
                    for k in range(2):
                        for j in range(QB):
                            mm = pe.transpose(bank16(4)[:, (k * QB + j) * P:(k * QB + j + 1) * P],
                                              hl[:, QB * q + j, k * D:k * D + D], ident16[:, :])
                    mm.then_inc(s_hTp, 1)
                for q in range(q0, q1):
                    pe.wait_ge(s_hT, q + 1)
                    if g >= 1 and q == q0:
                        pe.wait_ge(s_idx[0], g)
                    for j in range(QB):
                        b = QB * q + j
                        o = bank(5)[:, (b - g * NT) * ER:(b - g * NT + 1) * ER]
                        th, tl = hT[:, 0, b * P:b * P + P], hT[:, 1, b * P:b * P + P]
                        pe.matmul(o, th, r0h[:, 0, :], start=True, stop=False, skip_group_check=True)
                        pe.matmul(o, th, r0h[:, 1, :], start=False, stop=False, skip_group_check=True)
                        mm = pe.matmul(o, tl, r0h[:, 0, :], start=False, stop=True, skip_group_check=True)
                mm.then_inc(s_lg[0], 1)
                rank_mm(0, g)

            def shared_up(k, j):
                n = 2 * k + j
                if n >= 2:
                    pe.wait_ge(s_sS, n - 1)
                e = ER + j
                for c in range(FC):
                    o = bank(2 + 2 * j + c)
                    wh = rec0[:, e, W1_HI + c * P:W1_HI + c * P + P]
                    wl = rec0[:, e, W1_LO + c * P:W1_LO + c * P + P]
                    th = hT[:, 0, k * 512:(k + 1) * 512]
                    tl = hT[:, 1, k * 512:(k + 1) * 512]
                    pe.matmul(o, wh, th, start=True, stop=False)
                    pe.matmul(o, wh, tl, start=False, stop=False)
                    mm = pe.matmul(o, wl, th, start=False, stop=True)
                mm.then_inc(s_sU, 1)

            def shared_down(k):
                pe.wait_ge(s_sLo, 2 * k + 2)
                if k >= 2:
                    pe.wait_ge(s_sY, k - 1)
                for t in range(QB):
                    o = bank(6 + k % 2)[:, t * D:t * D + D]
                    first = True
                    for j in range(ES):
                        for c in range(FC):
                            at = W2_AT + 2 * D * c
                            w2h, w2l = rec0[:, ER + j, at:at + D], rec0[:, ER + j, at + D:at + 2 * D]
                            h_, l_ = (v[:, j, c * 512 + t * P:c * 512 + t * P + P] for v in (hh, hlo))
                            pe.matmul(o, h_, w2h, start=first, stop=False, skip_group_check=True)
                            pe.matmul(o, h_, w2l, start=False, stop=False, skip_group_check=True)
                            mm = pe.matmul(o, l_, w2h, start=False, stop=(j == ES - 1 and c == FC - 1),
                                           skip_group_check=True)
                            first = False
                mm.then_inc(s_sD, 1)

            pe.wait_ge(s_rec0, E0)
            pe.wait_ge(s_pooled, NQ)
            pe.wait_ge(s_idx[0], G)
            for k in range(NQ + 1):
                if k < NQ:
                    for j in range(ES):
                        shared_up(k, j)
                if k >= 1:
                    shared_down(k - 1)

            def tile_T(l, n, slot, b):
                s = L[l]
                pe.wait_ge(s["rows"][slot // 2], 16 * (n_turn(n) + 1))
                pe.wait_ge(s["xt"], val(n) + 3)
                for k in range(2):
                    for h in range(HALVES):
                        mm = pe.transpose(bank16(b)[:, (k * HALVES + h) * P:(k * HALVES + h + 1) * P],
                                          rowr[:, slot, h, k * D:k * D + D], ident16[:, :])
                mm.then_inc(s["T"], 1)

            def val(n):
                return n[0]

            def n_turn(n):
                return n[1]

            def tile_U(l, n, slot, b):
                s = L[l]
                pe.wait_ge(s["xt"], val(n) + 1 + CREDIT)
                pe.wait_ge(s["w"][slot], 16 * (n_turn(n) + 1))
                pe.wait_ge(s["silu" if l == 0 else "h"], val(n) + 3)
                for m in range(1 + l):
                    for c in range(FC):
                        o = bank(2 + 2 * b + m)[:, c * SLOTS:(c + 1) * SLOTS]
                        at = 2 * F * m + c * P
                        wh, wl = wr[:, slot, at:at + P], wr[:, slot, at + F:at + F + P]
                        pe.matmul(o, wh, xt[:, b, 0, :], start=True, stop=False, skip_group_check=True)
                        pe.matmul(o, wh, xt[:, b, 1, :], start=False, stop=False, skip_group_check=True)
                        mm = pe.matmul(o, wl, xt[:, b, 0, :], start=False, stop=True, skip_group_check=True)
                mm.then_inc(s["U"], 1)

            def tile_D(l, n, slot, b):
                s = L[l]
                pe.wait_ge(s["lo"], val(n) + 1 + CREDIT)
                pe.wait_ge(s["y"], val(n) + 3)
                at0 = W2_AT if l == 0 else DN_AT
                for h in range(HALVES):
                    o = bank(6 + b)[:, h * D:h * D + D]
                    for c in range(FC):
                        at = at0 + 2 * D * c
                        w2h, w2l = wr[:, slot, at:at + D], wr[:, slot, at + D:at + 2 * D]
                        f = c * SLOTS + h * P
                        pe.matmul(o, hh4[:, slot, f:f + P], w2h, start=(c == 0), stop=False, skip_group_check=True)
                        pe.matmul(o, hh4[:, slot, f:f + P], w2l, start=False, stop=False, skip_group_check=True)
                        mm = pe.matmul(o, hlo4[:, slot, f:f + P], w2h, start=False,
                                       stop=(c == FC - 1 and l == 0), skip_group_check=True)
                    if l == 1:
                        mm = pe.matmul(o, ones16[:, :], wr[:, slot, DB_AT:DB_AT + D], start=False, stop=True,
                                       skip_group_check=True)
                mm.then_inc(s["D"], 1)

            def tiles(l, g):
                base, tm = g * TM[l], TM[l]

                def num(i):
                    return (base + i, (base + i) // WRING), (base + i) % WRING, (base + i) % 2

                def step(i):
                    if i + 1 < tm:
                        n, slot, b = num(i + 1)
                        tile_T(l, n, slot, b)
                    if i >= 2:
                        n, slot, b = num(i - 2)
                        tile_D(l, n, slot, b)
                    if 0 <= i < tm:
                        n, slot, b = num(i)
                        tile_U(l, n, slot, b)
                for i in range(-1, 2):
                    step(i)
                loops = (tm - 3) // WRING
                with pe.Fori(0, loops) as turn:
                    for j in range(WRING):
                        def at(d):
                            k = base + 2 + j + d
                            return (WRING * turn + k, turn + k // WRING), k % WRING, k % 2
                        tile_T(l, *at(1))
                        tile_D(l, *at(-2))
                        tile_U(l, *at(0))
                for i in range(2 + loops * WRING, tm + 2):
                    step(i)

            pe.wait_ge(s_sY, NQ)
            for g in range(G):
                tiles(0, g)
            pe.wait_ge(s_iscat, 1)
            pe.wait_ge(L[0]["y"], G * TM[0] + CREDIT)

            def front1(g):
                for t in range(NT + 5):
                    n = g * NT + t - 1
                    if 0 <= t - 1 < NT:
                        pe.wait_ge(s_xlo, n + 1)
                        if n >= 2:
                            pe.wait_ge(s_xtt, n - 1)
                        for k in range(2):
                            mm = pe.transpose(bank16(n % 2)[:, k * P:k * P + P], xs16[:, n % 2, k * D:k * D + D],
                                              ident16[:, :])
                        mm.then_inc(s_t2, 1)
                    n = g * NT + t - 4
                    if 0 <= t - 4 < NT:
                        pe.wait_ge(s_clo, n + 1)
                        if n >= 2:
                            pe.wait_ge(s_ctt, n - 1)
                        for k in range(2):
                            mm = pe.transpose(bank16(4 + n % 2)[:, k * P:k * P + P], hl[:, n, k * D:k * D + D],
                                              ident16[:, :])
                        mm.then_inc(s_t3, 1)
                    n = g * NT + t - 2
                    if 0 <= t - 2 < NT:
                        pe.wait_ge(s_xtt, n + 1)
                        if n >= 2:
                            pe.wait_ge(s_clo, n - 1)
                        o = bank(2 + n % 2)[:, 0:D]
                        pe.matmul(o, xtt[:, n % 2, 0:P], wc[:, n, 0:D], start=True, stop=False)
                        pe.matmul(o, xtt[:, n % 2, 0:P], wc[:, n, D:2 * D], start=False, stop=False)
                        pe.matmul(o, xtt[:, n % 2, P:2 * P], wc[:, n, 0:D], start=False, stop=False)
                        pe.matmul(o, is_cat[:, n:n + 1].broadcast_to([NC, P]), cbt[:, :], start=False,
                                  stop=True).then_inc(s_c, 1)
                    n = g * NT + t - 5
                    if 0 <= t - 5 < NT:
                        pe.wait_ge(s_ctt, n + 1)
                        if g >= 1 and t == 5:
                            pe.wait_ge(s_idx[1], g)
                        o = bank(6)[:, (t - 5) * E1:(t - 4) * E1]
                        pe.matmul(o, ctt[:, n % 2, 0:P], r1h[:, 0, :], start=True, stop=False, skip_group_check=True)
                        pe.matmul(o, ctt[:, n % 2, 0:P], r1h[:, 1, :], start=False, stop=False, skip_group_check=True)
                        mm = pe.matmul(o, ctt[:, n % 2, P:2 * P], r1h[:, 0, :], start=False, stop=True,
                                       skip_group_check=True)
                        mm.then_inc(s_lg[1], 1)
                rank_mm(1, g)

            for g in range(G):
                front1(g)
            pe.wait_ge(s_idx[1], G)
            for g in range(G):
                tiles(1, g)

        @block.scalar
        def _(act):
            chain = [0]

            def link(ins):
                chain[0] += 1
                ins.then_inc(s_act, 1)
                act.wait_ge(s_act, chain[0])

            def copy_xT(q):
                act.wait_ge(s_xTp, q + 1)
                nc.scalar.copy(xT[:, q * QB * P:(q + 1) * QB * P], bank(q % 2)).then_inc(s_xT, 1)

            def route_act(l, g):
                e = NEXP[l]
                act.wait_ge(s_diff[l], g + 1)
                nc.scalar.activation(ex[:, :, 0:e], dd[:, :, 0:e], ACT.Exp, scale=INV)
                nc.scalar.activation(sm[:, 1, :], sm[:, 0, :], ACT.Exp, scale=INV).then_inc(s_ex[l], 1)

            for g in range(4):
                act.dma_start(brep[32 * g:32 * g + 32, :], cb1.rearrange("(a o) -> a o", o=1)).then_inc(s_av, 16)
                act.dma_start(vrep[32 * g:32 * g + 32, :], cv.rearrange("(a o) -> a o", o=1)).then_inc(s_av, 16)
            for q in range(NQ):
                copy_xT(q)
            act.wait_ge(s_av, 16 * 8)
            for h in range(2):
                act.wait_ge(s_pa, h + 1)
                nc.scalar.activation(attn[:, h, :], bank(2 + h), ACT.Tanh, bias=brep[:, 0:1]).then_inc(s_tanh, 1)

            def split0(e):
                if e == 0:
                    act.wait_ge(s_vcols, 2)
                act.wait_ge(s_raw0[e % RAWS], 32 * (e // RAWS + 1))
                nc.scalar.mul(rec0[:, e, W1_HI:W1_HI + F], raw0[:, e % RAWS, 0:F], vcols[:, e:e + 1])
                nc.scalar.mul(rec0[:, e, W2_AT:REC0].rearrange("p (c k n) -> p c k n", c=FC, k=2)[:, :, 0, :],
                              raw0[:, e % RAWS, F:2 * F].rearrange("p (c n) -> p c n", c=FC), WSCALE).then_inc(s_rec0hi, 1)

            act.wait_ge(s_sT, 1)
            for g in range(G):
                q0, q1 = g * NQ // G, (g + 1) * NQ // G

                def squares(q):
                    act.wait_ge(s_pooled, q + 1)
                    if q >= 1:
                        act.wait_ge(s_ssq, q)
                    for j in range(QB):
                        b = QB * q + j
                        ins = nc.scalar.activation(squares_out[:, j * D:j * D + D], pooled[:, b, :], ACT.Square,
                                                   accum_out=ssq[:, b:b + 1])
                    ins.then_inc(s_ssq, 1)
                for q in range(q0, q1):
                    act.wait_ge(s_arg, q + 1)
                    if q >= 2:
                        act.wait_ge(s_pool, q - 1)
                    for j in range(QB):
                        b = QB * q + j
                        ins = nc.scalar.activation(PT[:, q % 2, j * P:j * P + P], bank(6 + q % 2)[:, j * P:j * P + P],
                                                   ACT.Exp, bias=sT[:, b:b + 1], scale=-1.0)
                    ins.then_inc(s_pt, 1)
                    split0(2 * q)
                    split0(2 * q + 1)
                    if q > q0:
                        squares(q - 1)
                squares(q1 - 1)
                gs = slice(g * NT, (g + 1) * NT)
                act.wait_ge(s_ms, g + 1)
                nc.scalar.activation(sq[:, gs], rr[:, gs], ACT.Sqrt).then_inc(s_sqrt, 1)
                for q in range(q0, q1):
                    act.wait_ge(s_h0, q + 1)
                    nc.scalar.copy(hl[:, QB * q:QB * q + QB, 0:D], pooled[:, QB * q:QB * q + QB, :]).then_inc(s_hhi, 1)
                route_act(0, g)

            def shared_silu(n):
                act.wait_ge(s_sU, n + 1)
                if n >= 2:
                    act.wait_ge(s_sLo, n - 1)
                j = n % 2
                nc.scalar.activation(hf[:, j, :].rearrange("p (c t) -> p c t", c=FC), ps[:, 2 + 2 * j:4 + 2 * j, :],
                                     ACT.Silu, scale=INV).then_inc(s_sS, 1)

            def split_w(e):
                act.wait_ge(s_raw1[e % 2], 16 * 7 * (e // 2 + 1))
                r = raw1[:, e % 2, :]
                nc.scalar.mul(rec1[:, e, 0:4 * F].rearrange("p (m k f) -> p m k f", m=2, k=2)[:, :, 0, :],
                              r[:, 0:2 * F].rearrange("p (m f) -> p m f", m=2), WSCALE)
                nc.scalar.mul(rec1[:, e, DN_AT:BIAS_AT].rearrange("p (c k n) -> p c k n", c=FC, k=2)[:, :, 0, :],
                              r[:, 2 * F:3 * F].rearrange("p (c n) -> p c n", c=FC), WSCALE)
                nc.scalar.mul(wc[:, 4 * e:4 * e + 4, 0:D], r[:, 3 * F:].rearrange("p (b n) -> p b n", b=4),
                              WSCALE).then_inc(s_rec1hi, 1)

            nc.scalar.preload_act_table(ACT.Silu)
            act.wait_ge(s_zfill, 16 * G)
            for k in range(NQ):
                shared_silu(2 * k)
                split_w(k)
                shared_silu(2 * k + 1)

            def tiles(l, g):
                s = L[l]
                base, tm = g * TM[l], TM[l]

                def copy_x(n, b):
                    act.wait_ge(s["T"], n + 1 + CREDIT)
                    act.wait_ge(s["U"], n + 3)
                    nc.scalar.copy(xt[:, b, :, :].rearrange("p k s -> p (k s)"),
                                   bank16(b)[:, 0:2 * SLOTS]).then_inc(s["xt"], 1)

                def silu(n, b, slot):
                    act.wait_ge(s["U"], n + 1 + CREDIT)
                    act.wait_ge(s["lo"], n + 3)
                    if l == 0:
                        nc.scalar.activation(hf[:, b, 0:FC * SLOTS], bank(2 + 2 * b), ACT.Silu,
                                             scale=INV).then_inc(s["silu"], 1)
                    else:
                        for c in range(FC):
                            ins = nc.scalar.activation(hf[:, b, (2 + c) * SLOTS:(3 + c) * SLOTS],
                                                       bank(2 + 2 * b)[:, c * SLOTS:(c + 1) * SLOTS], ACT.Silu,
                                                       bias=bias_of(slot, c), scale=INV)
                        ins.then_inc(s["silu"], 1)

                def y_copy(n, k, turn):
                    act.wait_ge(s["D"], n + 1 + CREDIT)
                    if k % 2 == 0:
                        act.wait_ge(s["st"][k // 2 % 2], 16 * (k // 4 + turn + 1))
                    nc.scalar.copy(ys[:, k % YRING, :, :].rearrange("p h d -> p (h d)"),
                                   bank(6 + k % 2)[:, 0:HALVES * D]).then_inc(s["y"], 1)

                def store(i, n, k):
                    act.wait_ge(s["y"], n + 1 + CREDIT)
                    pair = k // 2 % (YRING // 2)
                    act.dma_start(y_d[g].rearrange("(t h p) d -> t p h d", h=2 * HALVES, p=P)[bass.ds(i, 1)].rearrange(
                        "a p h d -> (a p) h d"),
                        ys[:, 2 * pair:2 * pair + 2, :, :].rearrange("p t h d -> p (t h) d")).then_inc(s["st"][pair], 16)

                def load_rows(g, p, turn):
                    loop = type(turn) is not int
                    off = WRING * turn if loop else 0
                    base = g * TM[l]
                    if p == 0:
                        act.wait_ge(s_scat[l][g], 16 * 2 * NT)
                    pair = (base + p) // 2 % (RRING // 2)
                    act.wait_ge(s["T"], base + p + 2 + off)
                    act.dma_start(rowr[:, 2 * pair:2 * pair + 2, :, :].rearrange("p t h c -> p (t h) c"),
                                  rows_d[g].rearrange("(t h p) c -> t p h c", h=2 * HALVES, p=P)[
                                      bass.ds(p // 2 + (WRING // 2 * turn if loop else 0), 1)].rearrange(
                                          "a p h c -> (a p) h c")).then_inc(s["rows"][pair], 16)

                def step(i0, turn):
                    loop = type(turn) is not int
                    off = WRING * turn if loop else 0

                    def ok(d):
                        return loop or 0 <= i0 + d < tm
                    if ok(1):
                        n = base + i0 + 1
                        copy_x(n + off, n % 2)
                    n = base + i0 - 2
                    if ok(-2) and l == 1:
                        y_copy(n + off, n, turn)
                    if ok(0):
                        silu(n + 2 + off, n % 2, (n + 2) % WRING)
                    if ok(1) and (n + 3) % 2 == 1:
                        if loop or i0 + 4 < tm:
                            load_rows(g, i0 + 4, turn)
                        elif g + 1 < G:
                            load_rows(g + 1, i0 + 4 - tm, 0)
                    if ok(-2) and n % 2 == 1:
                        store((i0 - 3) // 2 + (WRING // 2 * turn if loop else 0), n + off, n)
                if g == 0:
                    load_rows(0, 0, 0)
                    load_rows(0, 2, 0)
                for i in range(-1, 2):
                    step(i, 0)
                loops = (tm - 6) // WRING
                with act.Fori(0, loops) as turn:
                    for j in range(WRING):
                        step(2 + j, turn)
                for i in range(2 + loops * WRING, tm + 2):
                    step(i, 0)

            def bias_of(slot, k):
                return wr[:, slot, BIAS_AT + 2 * k:BIAS_AT + 2 * k + 2].bitcast(F32)

            for g in range(G):
                tiles(0, g)

            def front1(g):
                for t in range(NT + 3):
                    n = g * NT + t
                    if t < NT:
                        act.wait_ge(s_x1, n + 1)
                        if n >= 2:
                            act.wait_ge(s_t2, n - 1)
                        nc.scalar.copy(xs16[:, n % 2, 0:D], xs[:, n, 0:D]).then_inc(s_xhi, 1)
                    n = g * NT + t - 2
                    if 0 <= t - 2 < NT:
                        act.wait_ge(s_t2, n + 1)
                        if n >= 2:
                            act.wait_ge(s_c, n - 1)
                        nc.scalar.copy(xtt[:, n % 2, :], bank16(n % 2)[:, 0:2 * P]).then_inc(s_xtt, 1)
                    n = g * NT + t - 3
                    if 0 <= t - 3 < NT:
                        act.wait_ge(s_c, n + 1)
                        if t == 3:
                            act.wait_ge(s_scat[0][g], 16 * 2 * NT)
                        nc.scalar.mul(hl[:, n, 0:D], bank(2 + n % 2)[:, 0:D], INV).then_inc(s_chi, 1)
                route_act(1, g)

            for g in range(G):
                front1(g)
            nc.scalar.preload_act_table(ACT.Silu)
            for g in range(G):
                tiles(1, g)

        @block.vector
        def _(dve):
            v = nc.vector
            chain = [0]

            def link(ins):
                chain[0] += 1
                ins.then_inc(s_dve, 1)
                dve.wait_ge(s_dve, chain[0])

            dve.wait_ge(s_const, 16)
            v.tensor_copy(ident16[:, :], ident)
            v.tensor_copy(identb[:, :], ident)
            v.tensor_copy(deltab[:, :], delta32)
            link(v.tensor_copy(ustrict16[:, :], cst[:, C_USTRICT:C_USTRICT + P]))
            dve.wait_ge(s_small, 16 * 3)
            dve.wait_ge(s_av, 16 * 8)
            dve.wait_ge(s_pads, 6)
            v.tensor_scalar(vsel[:, :], cst[:, C_VMASK:NCONST], vrep[:, 0:1], None, ALU.mult).then_inc(s_vsel, 1)
            link(v.tensor_scalar(selc[:, 0:1], ptc[:, :], 0.0, None, ALU.is_equal))
            link(v.tensor_scalar(selc[:, 1:2], ptc[:, :], 1.0, None, ALU.is_equal))
            link(v.tensor_tensor(selc[:, 3:4], selc[:, 0:1], selc[:, 1:2], ALU.add))
            link(v.tensor_scalar(selc[:, 2:3], selc[:, 3:4], -1.0, 1.0, ALU.mult, ALU.add))
            v.tensor_scalar(selb[:, 0, :], ptb[:, :], 0.0, None, ALU.is_equal)
            link(v.tensor_scalar(selb[:, 1, :], ptb[:, :], 1.0, None, ALU.is_equal))
            link(v.tensor_tensor(selb[:, 3, :], selb[:, 0, :], selb[:, 1, :], ALU.add))
            link(v.tensor_scalar(selb[:, 2, :], selb[:, 3, :], -1.0, 1.0, ALU.mult, ALU.add))
            link(v.tensor_scalar(cnt[:, :], selb[:, 0, :], cst[:, C_CNT:C_CNT + 1], None, ALU.mult))
            link(v.scalar_tensor_tensor(cnt[:, :], selb[:, 1, :], cst[:, C_CNT + 1:C_CNT + 2], cnt[:, :],
                                        ALU.mult, ALU.add))
            link(v.scalar_tensor_tensor(cnt[:, :], selb[:, 2, :], cst[:, C_CNT + 2:C_CNT + 3], cnt[:, :],
                                        ALU.mult, ALU.add))
            link(v.tensor_tensor(selb[:, 3, :], selb[:, 0, :], selb[:, 1, :], ALU.subtract))
            link(v.tensor_scalar(selb[:, 3, :], selb[:, 3, :], BIG, None, ALU.mult))
            link(v.tensor_scalar(selb[:, 2, :], selb[:, 2, :], BIG, None, ALU.mult))

            def masks(q):
                if q >= 2:
                    dve.wait_ge(s_arg, q - 1)
                for j in range(QB):
                    b = QB * q + j
                    v.tensor_scalar(mk[:, q % 2, 0, j * P:j * P + P], deltab[:, :], selb[:, 3, b:b + 1], 0.0,
                                    ALU.mult, ALU.max)
                    ins = v.tensor_scalar(mk[:, q % 2, 1, j * P:j * P + P], identb[:, :], selb[:, 2, b:b + 1],
                                          None, ALU.mult)
                ins.then_inc(s_mk, 1)


            def split0(e):
                dve.wait_ge(s_rec0hi, e + 1)
                v.scalar_tensor_tensor(rec0[:, e, W1_LO:W1_LO + F], raw0[:, e % RAWS, 0:F], vcols[:, e:e + 1],
                                       rec0[:, e, W1_HI:W1_HI + F], ALU.mult, ALU.subtract)
                w2v = rec0[:, e, W2_AT:REC0].rearrange("p (c k n) -> p c k n", c=FC, k=2)
                v.scalar_tensor_tensor(w2v[:, :, 1, :], raw0[:, e % RAWS, F:2 * F].rearrange("p (c n) -> p c n", c=FC),
                                       WSCALE, w2v[:, :, 0, :], ALU.mult, ALU.subtract).then_inc(s_rec0, 1)

            masks(0)
            masks(1)
            dve.wait_ge(s_sc, 1)
            v.tensor_copy(ssb[:, :], bank(4)[0:B, 0:P]).then_inc(s_ssb, 1)
            mid = 64
            dve.wait_ge(s_ssb, 1)
            v.tensor_copy(mx[:, 0, mid:mid + P], ssb[:, :])
            link(v.tensor_copy(mx[:, 2, mid:mid + P], ssb[:, :]))
            at = 0
            for k in range(7):
                s = 1 << k
                v.tensor_tensor(mx[:, 1 - at, mid:mid + P], mx[:, at, mid:mid + P], mx[:, at, mid - s:mid - s + P],
                                ALU.max)
                link(v.tensor_tensor(mx[:, 3 - at, mid:mid + P], mx[:, 2 + at, mid:mid + P],
                                     mx[:, 2 + at, mid + s:mid + s + P], ALU.max))
                at = 1 - at
            dve.wait_ge(s_sTp, 1)
            v.tensor_copy(sT[:, :], bank(5)[:, 0:B]).then_inc(s_sT, 1)
            left, right, both = mx[:, at, :], mx[:, 2 + at, :], mx[:, 1 - at, mid:mid + P]
            link(v.tensor_scalar(mrow[:, :], left[:, mid:mid + P], selc[:, 0:1], None, ALU.mult))
            link(v.scalar_tensor_tensor(mrow[:, :], right[:, mid:mid + P], selc[:, 1:2], mrow[:, :],
                                        ALU.mult, ALU.add))
            link(v.tensor_tensor(both, left[:, mid - 1:mid - 1 + P], right[:, mid + 1:mid + 1 + P], ALU.max))
            v.scalar_tensor_tensor(mrow[:, :], both, selc[:, 2:3], mrow[:, :], ALU.mult, ALU.add).then_inc(s_max, 1)
            dve.wait_ge(s_vt, 1)
            v.tensor_copy(vcols[:, :], bank(4)[:, 0:56]).then_inc(s_vcols, 1)
            dve.wait_ge(s_vcols, 1)
            v.tensor_scalar(vcols[:, 0:E0], vcols[:, 0:E0], WSCALE, None, ALU.mult).then_inc(s_vcols, 1)
            dve.wait_ge(s_late, 16 * 10)
            link(v.tensor_scalar(is_cat[:, :], catb[:, :], 1.0, None, ALU.add))
            v.tensor_scalar(is_cat[:, :], is_cat[:, :], cst[0:NC, C_CNT:C_CNT + 1], WSCALE, ALU.is_equal,
                            ALU.mult).then_inc(s_iscat, 1)
            link(v.tensor_scalar(r0h[:, 0, :], r0s[:, :], WSCALE, None, ALU.mult))
            v.scalar_tensor_tensor(r0h[:, 1, :], r0s[:, :], WSCALE, r0h[:, 0, :], ALU.mult, ALU.subtract)
            dve.wait_ge(s_vcols, 1)
            link(v.tensor_scalar(r1h[:, 0, :], vcols[:, 48:56], WSCALE, None, ALU.mult))
            v.scalar_tensor_tensor(r1h[:, 1, :], vcols[:, 48:56], WSCALE, r1h[:, 0, :], ALU.mult, ALU.subtract)
            bias = rec1[:, :, BIAS_AT:DB_AT].bitcast(F32)
            v.tensor_copy(bias[:, :, 0:FC], vcols[:, 16:32].rearrange("p (e c) -> p e c", c=FC))
            v.tensor_scalar(bias[:, :, FC:2 * FC], vcols[:, 32:48].rearrange("p (e c) -> p e c", c=FC),
                            WSCALE, None, ALU.mult)
            v.tensor_scalar(dbh[:, 0, :], dbr[:, :], WSCALE, None, ALU.mult).then_inc(s_db, 1)
            dve.wait_ge(s_db, 1)
            v.scalar_tensor_tensor(dbh[:, 1, :], dbr[:, :], WSCALE, dbh[:, 0, :], ALU.mult,
                                   ALU.subtract).then_inc(s_db, 1)

            def copy_hT(q):
                dve.wait_ge(s_hTp, q + 1)
                v.tensor_copy(hT[:, :, q * QB * P:(q + 1) * QB * P],
                              bank16(4).rearrange("p (k t) -> p k t", k=2)).then_inc(s_hT, 1)

            def route(l, g):
                e, tm = NEXP[l], TM[l]
                gs = slice(g * NT, (g + 1) * NT)

                def over(a):
                    return a.unsqueeze(2).broadcast_to([P, NT, e])

                lge, dde, d2e, cde = lg[:, :, 0:e], dd[:, :, 0:e], d2[:, :, 0:e], cd[:, :, 0:e]
                iota = cst[:, C_IOTA:C_IOTA + e].unsqueeze(1).broadcast_to([P, NT, e])
                m2, e2x, mtop, code, zs, g1, g2, den = (sm[:, i, :] for i in range(8))
                if l == 0:
                    dve.wait_ge(s_lg[0], g + 1)
                    link(v.tensor_tensor(lge, bank(5)[:, 0:NT * e].rearrange("p (t e) -> p t e", e=e),
                                         over(sq[:, gs]), ALU.mult))
                else:
                    dve.wait_ge(s_lg[1], (g + 1) * NT)
                    link(v.tensor_copy(lge, bank(6)[:, 0:NT * e].rearrange("p (t e) -> p t e", e=e)))
                link(v.tensor_reduce(mtop, lge, AX.X, ALU.max))
                link(v.tensor_tensor(dde, lge, over(mtop), ALU.subtract))
                link(v.scalar_tensor_tensor(cde, dde, 0.0, iota, ALU.is_equal, ALU.mult))
                link(v.tensor_reduce(code, cde, AX.X, ALU.min))
                link(v.tensor_tensor(oh1[:, :, 0:e], iota, over(code), ALU.is_equal))
                link(v.scalar_tensor_tensor(d2e, oh1[:, :, 0:e], LOW, dde, ALU.mult, ALU.add))
                v.tensor_reduce(m2, d2e, AX.X, ALU.max).then_inc(s_diff[l], 1)
                dve.wait_ge(s_diff[l], g + 1)
                link(v.tensor_tensor(d2e, d2e, over(m2), ALU.subtract))
                link(v.scalar_tensor_tensor(cde, d2e, 0.0, iota, ALU.is_equal, ALU.mult))
                link(v.tensor_reduce(code, cde, AX.X, ALU.min))
                link(v.tensor_tensor(oh2[:, :, 0:e], iota, over(code), ALU.is_equal))
                v.tensor_tensor(oh16[:, :, 0:e], oh1[:, :, 0:e], oh2[:, :, 0:e], ALU.add).then_inc(s_oh[l], 1)
                dve.wait_ge(s_ex[l], g + 1)
                link(v.tensor_reduce(zs, ex[:, :, 0:e], AX.X, ALU.add))
                link(v.reciprocal(g1, zs))
                link(v.tensor_tensor(g2, e2x, g1, ALU.mult))
                link(v.tensor_tensor(den, g1, g2, ALU.add))
                link(v.tensor_scalar(den, den, 1e-9, None, ALU.add))
                link(v.reciprocal(den, den))
                v.scalar_tensor_tensor(gwt[:, l, 0, gs], g1, INV, den, ALU.mult, ALU.mult)
                link(v.scalar_tensor_tensor(gwt[:, l, 1, gs], g2, INV, den, ALU.mult, ALU.mult))
                dve.wait_ge(s_rank[l], g + 1)
                rb = rank_bank(l)
                link(v.tensor_copy(pre[:, 0, 16:16 + NT, 0:e],
                                   rb[:, 256:256 + NT * e].rearrange("p (t e) -> p t e", e=e)))
                at, s = 0, 1
                while s < NT:
                    link(v.tensor_tensor(pre[:, 1 - at, 16:16 + NT, 0:e], pre[:, at, 16:16 + NT, 0:e],
                                         pre[:, at, 16 - s:16 + NT - s, 0:e], ALU.add))
                    at, s = 1 - at, 2 * s
                link(v.tensor_scalar(nti[:, 0, 0:e], pre[:, at, 15 + NT, 0:e], SLOTS - 1.0, None, ALU.add))
                link(v.tensor_scalar(nti[:, 1, 0:e], nti[:, 0, 0:e], SLOTS.bit_length() - 1, None,
                                     ALU.logical_shift_right))
                link(v.tensor_copy(ntf[:, 0, 16:16 + e], nti[:, 1, 0:e]))
                a2, s = 0, 1
                while s < e:
                    link(v.tensor_tensor(ntf[:, 1 - a2, 16:16 + e], ntf[:, a2, 16:16 + e],
                                         ntf[:, a2, 16 - s:16 + e - s], ALU.add))
                    a2, s = 1 - a2, 2 * s
                upto = ntf[:, a2, :]
                tau = cst[0:1, C_TILE:C_TILE + tm].unsqueeze(2).broadcast_to([1, tm, e])
                ends = upto[0:1, 16:16 + e].unsqueeze(1).broadcast_to([1, tm, e])
                link(v.tensor_tensor(cmp_[:, 0:tm, 0:e], tau, ends, ALU.is_ge))
                link(v.tensor_reduce(tef[:, 0, 0:tm], cmp_[:, 0:tm, 0:e], AX.X, ALU.add))
                link(v.tensor_scalar(tef[:, 1, 0:tm], tef[:, 0, 0:tm], e - 1.0, None, ALU.min))
                link(v.tensor_copy(te[:, l, g, 0:tm], tef[:, 1, 0:tm]))
                link(v.tensor_scalar(cmp_base[:, 0:e], upto[:, 15:15 + e], float(SLOTS), None, ALU.mult))
                link(v.tensor_tensor(lge, rb[:, 0:NT * e].rearrange("p (t e) -> p t e", e=e),
                                     pre[:, at, 15:15 + NT, 0:e], ALU.add))
                link(v.tensor_tensor(lge, lge, cmp_base[:, 0:e].unsqueeze(1).broadcast_to([P, NT, e]), ALU.add))
                for k, oh in enumerate((oh1, oh2)):
                    link(v.tensor_tensor(cde, lge, oh[:, :, 0:e], ALU.mult))
                    link(v.tensor_reduce(sm[:, 8 + k, :], cde, AX.X, ALU.add))
                v.tensor_copy(idx[:, l, 0, gs], sm[:, 8, :])
                v.tensor_copy(idx[:, l, 1, gs], sm[:, 9, :]).then_inc(s_idx[l], 1)
                dve.wait_ge(s_idx[l], g + 1)

            for g in range(G):
                q0, q1 = g * NQ // G, (g + 1) * NQ // G
                for q in range(q0, q1):
                    if q + 2 < NQ:
                        masks(q + 2)
                    dve.wait_ge(s_pool, q + 1)
                    o = ps[:, 2 * (q % 2):2 * (q % 2) + 2, :].rearrange("p a (b c) -> p a b c", b=2)
                    bs = slice(QB * q, QB * q + QB)
                    link(v.tensor_tensor(rc[:, bs].rearrange("p (a b) -> p a b", a=2), o[:, :, :, D],
                                         cnt[:, bs].rearrange("p (a b) -> p a b", a=2), ALU.mult))
                    link(v.reciprocal(rc[:, bs], rc[:, bs]))
                    v.tensor_tensor(pooled[:, bs, :].rearrange("p (a b) d -> p a b d", a=2), o[:, :, :, 0:D],
                                    rc[:, bs].rearrange("p (a b) -> p a b", a=2).unsqueeze(3).broadcast_to([P, 2, 2, D]),
                                    ALU.mult).then_inc(s_pooled, 1)
                    split0(2 * q)
                    split0(2 * q + 1)
                gs = slice(g * NT, (g + 1) * NT)
                dve.wait_ge(s_ssq, q1)
                v.tensor_scalar(rr[:, gs], ssq[:, gs], 1.0 / D, 1.1920929e-07, ALU.mult, ALU.add).then_inc(s_ms, 1)
                dve.wait_ge(s_sqrt, g + 1)
                link(v.reciprocal(rr[:, gs], sq[:, gs]))

                def normalise(q):
                    bs = slice(QB * q, QB * q + QB)
                    v.tensor_tensor(pooled[:, bs, :], pooled[:, bs, :],
                                    rr[:, bs].unsqueeze(2).broadcast_to([P, QB, D]), ALU.mult).then_inc(s_h0, 1)
                normalise(q0)
                for q in range(q0, q1):
                    if q + 1 < q1:
                        normalise(q + 1)
                    bs = slice(QB * q, QB * q + QB)
                    dve.wait_ge(s_hhi, q + 1)
                    v.tensor_tensor(hl[:, bs, D:2 * D], pooled[:, bs, :], hl[:, bs, 0:D],
                                    ALU.subtract).then_inc(s_hlo, 1)
                    if q > q0:
                        copy_hT(q - 1)
                copy_hT(q1 - 1)
                route(0, g)

            def shared_split(n):
                j, k = n % 2, n // 2
                dve.wait_ge(s_sS, n + 1)
                if k >= 1:
                    dve.wait_ge(s_sD, k)
                v.tensor_copy(hh[:, j, :], hf[:, j, :]).then_inc(s_sHi, 1)
                dve.wait_ge(s_sHi, n + 1)
                v.tensor_tensor(hlo[:, j, :], hf[:, j, :], hh[:, j, :], ALU.subtract).then_inc(s_sLo, 1)

            def shared_add(k):
                dve.wait_ge(s_sD, k + 1)
                xq = xs[:, QB * k:QB * k + QB, 0:D]
                v.scalar_tensor_tensor(xq, bank(6 + k % 2).rearrange("p (t d) -> p t d", d=D), INV, xq,
                                       ALU.mult, ALU.add).then_inc(s_sY, 1)

            def split_w(e):
                dve.wait_ge(s_rec1hi, e + 1)
                r = raw1[:, e % 2, :]
                gu = rec1[:, e, 0:4 * F].rearrange("p (m k f) -> p m k f", m=2, k=2)
                v.scalar_tensor_tensor(gu[:, :, 1, :], r[:, 0:2 * F].rearrange("p (m f) -> p m f", m=2), WSCALE,
                                       gu[:, :, 0, :], ALU.mult, ALU.subtract)
                dn = rec1[:, e, DN_AT:BIAS_AT].rearrange("p (c k n) -> p c k n", c=FC, k=2)
                v.scalar_tensor_tensor(dn[:, :, 1, :], r[:, 2 * F:3 * F].rearrange("p (c n) -> p c n", c=FC), WSCALE,
                                       dn[:, :, 0, :], ALU.mult, ALU.subtract)
                v.scalar_tensor_tensor(wc[:, 4 * e:4 * e + 4, D:2 * D], r[:, 3 * F:].rearrange("p (b n) -> p b n", b=4),
                                       WSCALE, wc[:, 4 * e:4 * e + 4, 0:D], ALU.mult, ALU.subtract).then_inc(s_rec1, 1)

            for k in range(NQ):
                shared_split(2 * k)
                shared_split(2 * k + 1)
                if k >= 1:
                    shared_add(k - 1)
                split_w(k)
            shared_add(NQ - 1)

            def tiles(l, g):
                s = L[l]
                base, tm = g * TM[l], TM[l]
                W = FC * SLOTS

                def split(n, slot, b):
                    dve.wait_ge(s["silu"], n + 1 + CREDIT)
                    h32 = hf[:, b, 0:W]
                    if l == 1:
                        for c in range(FC):
                            f = slice(c * SLOTS, (c + 1) * SLOTS)
                            ub_ = wr[:, slot, BIAS_AT + 2 * (FC + c):BIAS_AT + 2 * (FC + c) + 2].bitcast(F32)
                            ins = v.scalar_tensor_tensor(hf[:, b, f], bank(3 + 2 * b)[:, f], ub_,
                                                         hf[:, b, (2 + c) * SLOTS:(3 + c) * SLOTS], ALU.add, ALU.mult)
                        ins.then_inc(s["h"], 1)
                        dve.wait_ge(s["h"], n + 1 + CREDIT)
                    dve.wait_ge(s["D"], n + 1)
                    if l == 0:
                        v.tensor_copy(hh4[:, slot, 0:W], h32).then_inc(s["hi"], 1)
                    else:
                        v.tensor_scalar(hh4[:, slot, 0:W], h32, INV, None, ALU.mult).then_inc(s["hi"], 1)
                    dve.wait_ge(s["hi"], n + 1 + CREDIT)
                    if l == 0:
                        v.tensor_tensor(hlo4[:, slot, 0:W], h32, hh4[:, slot, 0:W], ALU.subtract).then_inc(s["lo"], 1)
                    else:
                        v.scalar_tensor_tensor(hlo4[:, slot, 0:W], h32, INV, hh4[:, slot, 0:W], ALU.mult,
                                               ALU.subtract).then_inc(s["lo"], 1)

                def y_copy(n, k, turn):
                    dve.wait_ge(s["D"], n + 1 + CREDIT)
                    if k % 2 == 0:
                        dve.wait_ge(s["st"][k // 2 % 2], 16 * (k // 4 + turn + 1))
                    v.tensor_copy(ys[:, k % YRING, :, :].rearrange("p h d -> p (h d)"),
                                  bank(6 + k % 2)[:, 0:HALVES * D]).then_inc(s["y"], 1)

                def step(i0, turn):
                    loop = type(turn) is not int
                    off = WRING * turn if loop else 0
                    n = base + i0 - 2
                    if l == 0 and (loop or i0 >= 2):
                        y_copy(n + off, n, turn)
                    if loop or i0 < tm:
                        split(n + 2 + off, (n + 2) % WRING, n % 2)
                for i in range(2):
                    step(i, 0)
                loops = (tm - 3) // WRING
                with dve.Fori(0, loops) as turn:
                    for j in range(WRING):
                        step(2 + j, turn)
                for i in range(2 + loops * WRING, tm + 2):
                    step(i, 0)

            for g in range(G):
                tiles(0, g)

            def combine(l, b):
                dve.wait_ge(s_gr[b // 2], 64 * (l + 1))
                xb = xs[:, b, 0:D]
                link(v.scalar_tensor_tensor(xb, gathered(l, b)[:, 0, :], gwt[:, l, 0, b:b + 1], xb, ALU.mult, ALU.add))
                v.scalar_tensor_tensor(xb, gathered(l, b)[:, 1, :], gwt[:, l, 1, b:b + 1], xb,
                                       ALU.mult, ALU.add).then_inc(s_x1, 1)

            def front1(g):
                for t in range(NT + 5):
                    n = g * NT + t
                    if t < NT:
                        combine(0, n)
                    n = g * NT + t - 1
                    if 0 <= t - 1 < NT:
                        dve.wait_ge(s_xhi, n + 1)
                        v.tensor_tensor(xs16[:, n % 2, D:2 * D], xs[:, n, 0:D], xs16[:, n % 2, 0:D],
                                        ALU.subtract).then_inc(s_xlo, 1)
                    n = g * NT + t - 4
                    if 0 <= t - 4 < NT:
                        dve.wait_ge(s_chi, n + 1)
                        v.scalar_tensor_tensor(hl[:, n, D:2 * D], bank(2 + n % 2)[:, 0:D], INV, hl[:, n, 0:D],
                                               ALU.mult, ALU.subtract).then_inc(s_clo, 1)
                    n = g * NT + t - 5
                    if 0 <= t - 5 < NT:
                        dve.wait_ge(s_t3, n + 1)
                        if n >= 2:
                            dve.wait_ge(s_lg[1], n - 1)
                        v.tensor_copy(ctt[:, n % 2, :], bank16(4 + n % 2)[:, 0:2 * P]).then_inc(s_ctt, 1)
                route(1, g)

            for g in range(G):
                front1(g)
            for g in range(G):
                tiles(1, g)
            for b in range(B):
                combine(1, b)


_INS = ['x', 'itok_B_0_2', 'itok_B_0_30', 'L0_cond_W1', 'L0_cond_b1', 'L0_cond_v', 'L0_ffn_router_w', 'L0_ffn_rms_w',
        'L0_ffn_w1', 'L0_ffn_w2', 'L0_ffn_rms_w_s', 'L0_ffn_w1_s', 'L0_ffn_w2_s', 'L1_cond_W', 'L1_cond_b',
        'L1_ffn_router_w', 'L1_ffn_gate_w', 'L1_ffn_gate_b', 'L1_ffn_up_w', 'L1_ffn_up_b', 'L1_ffn_down_w',
        'L1_ffn_down_b']


def kernel(**inputs):
    import concourse.bacc as bacc
    from concourse.bass_utils import run_bass_kernel_spmd

    nc = bacc.Bacc("TRN2", target_bir_lowering=False, num_devices=1)
    arrays, args = {}, []
    for name in _INS + ["constants"]:
        a = np.ascontiguousarray(constants() if name == "constants" else inputs[name])
        arrays[f"in_{name}"] = a
        args.append(nc.dram_tensor(f"in_{name}", a.shape, mybir.dt.from_np(a.dtype), kind="ExternalInput").ap())
    args.append(nc.dram_tensor("out_x", (B, P, D), F32, kind="ExternalOutput").ap())
    build(nc, *args)
    r = run_bass_kernel_spmd(nc, [arrays], core_ids=[0])
    return r.results[0]["out_x"]
```
